# Optimizing a Trainium2 kernel written in Bass

```python
import numpy as np
import jax
import jax.numpy as jnp

def _softmax(x, axis=-1):
    return jax.nn.softmax(x, axis=axis)

def _gelu(x):
    return jax.nn.gelu(x, approximate=True)

def _silu(x):
    return jax.nn.silu(x)

def _sigmoid(x):
    return jax.nn.sigmoid(x)

def _layernorm(x, axis=-1, eps=1e-05):
    m = jnp.mean(x, axis=axis, keepdims=True)
    v = jnp.var(x, axis=axis, keepdims=True)
    return (x - m) / jnp.sqrt(v + eps)

def _scatter_add(tgt, idx, src, axis=0):
    return tgt.at[idx].add(src)

def _segment_sum(src, seg, n):
    return jax.ops.segment_sum(src, seg, n)
kernel_name = 'mk_gnn_ffn_d1_gnn_r64_6fd303'

def setup_inputs(seed: int=0):
    np.random.seed(seed)
    _w = jnp.asarray

    def _rec_inputs():
        import jax
        import jax.numpy as jnp
        _gk = jax.random.key(seed)
        x = -0.000125 + 0.9999 * jax.random.normal(jax.random.fold_in(_gk, 1), (1024, 512), jnp.float32)
        src = jax.random.randint(jax.random.fold_in(_gk, 2), (16384,), 0, 1024, jnp.int32)
        dst = jnp.minimum((1024 * jax.random.uniform(jax.random.fold_in(_gk, 3), (16384,)) ** 2.0).astype(jnp.int32), 65535)
        _o = jnp.argsort(dst, stable=True)
        src = src[_o]
        dst = dst[_o]
        edge_weight = jax.random.uniform(jax.random.fold_in(_gk, 12), (16384,), jnp.float32, 0.0, 0.999998)
        return (x, src, dst, edge_weight)
    x, src, dst, edge_weight = _rec_inputs()

    def _L0_gnn_setup():
        import jax, jax.numpy as jnp
        import numpy as np
        N_NODES = 1024
        key = jax.random.key(seed)
        k1, k2, k3, k4, k5 = jax.random.split(key, 5)
        in_dim, out_dim, n_edges = (512, 512, 8192)
        H = jax.random.normal(k1, (N_NODES, in_dim), dtype=jnp.float32)
        stdv = 1.0 / np.sqrt(out_dim)
        W = jax.random.uniform(k2, (in_dim, out_dim), minval=-stdv, maxval=stdv, dtype=jnp.float32)
        bias = jnp.zeros((out_dim,), dtype=jnp.float32)
        edge_row = jax.random.randint(k3, (n_edges,), 0, N_NODES, dtype=jnp.int32)
        edge_col = jax.random.randint(k4, (n_edges,), 0, N_NODES, dtype=jnp.int32)
        edge_val = jax.random.uniform(k5, (n_edges,), dtype=jnp.float32)
        return {'H': H, 'W': W, 'bias': bias, 'edge_row': edge_row, 'edge_col': edge_col, 'edge_val': edge_val}
    _L0_gnn_all = _L0_gnn_setup()
    _L0_gnn_in = {k: v for k, v in _L0_gnn_all.items() if k in ('W', 'bias')}
    del _L0_gnn_all

    def _L0_ffn_setup():
        import jax, jax.numpy as jnp
        import numpy as np
        G = 4
        EPG = 4
        E = 16
        KG = 2
        K = 2
        GTP = 0.9
        TP = 0.9
        SCALE = 1.0 / float(np.sqrt(G))

        def _routing_weights(xf, Wr, br, Wgate, bgate):
            N = xf.shape[0]
            gp = jax.nn.softmax(xf @ Wr + br, axis=-1)
            order = jnp.argsort(-gp, axis=-1)
            sp_k = jnp.take_along_axis(gp, order, axis=-1)[:, :KG]
            idx_k = order[:, :KG]
            act = jnp.cumsum(sp_k, axis=-1) <= GTP
            act = act.at[:, 0].set(True)
            mp = sp_k * act
            rn = mp / (jnp.sum(mp, axis=-1, keepdims=True) + 1e-09)
            w_group = jnp.zeros((N, G), xf.dtype).at[jnp.arange(N)[:, None], idx_k].set(rn)
            ep = jax.nn.softmax(jnp.einsum('nd,gde->nge', xf, Wgate) + bgate, axis=-1)
            eorder = jnp.argsort(-ep, axis=-1)
            esp = jnp.take_along_axis(ep, eorder, axis=-1)[:, :, :K]
            eidx = eorder[:, :, :K]
            eact = jnp.cumsum(esp, axis=-1) <= TP
            eact = eact.at[:, :, 0].set(True)
            emp = esp * eact
            ern = emp / (jnp.sum(emp, axis=-1, keepdims=True) + 1e-09)
            w_exp = jnp.zeros((N, G, EPG), xf.dtype).at[jnp.arange(N)[:, None, None], jnp.arange(G)[None, :, None], eidx].set(ern)
            return (w_group[:, :, None] * w_exp * SCALE).reshape(N, E)
        key = jax.random.key(seed)
        ks = jax.random.split(key, 6)
        B, T, D, H = (2, 1024, 512, 32)
        x = jax.random.normal(ks[0], (B, T, D), jnp.float32)
        Wr = jax.random.normal(ks[1], (D, G), jnp.float32) * 0.02
        br = jnp.zeros((G,), jnp.float32)
        Wgate = jax.random.normal(ks[2], (G, D, EPG), jnp.float32) * 0.02
        bgate = jnp.zeros((G, EPG), jnp.float32)
        W1 = jax.random.normal(ks[3], (E, D, H), jnp.float32) * 0.02
        W3 = jax.random.normal(ks[4], (E, D, H), jnp.float32) * 0.02
        W2 = jax.random.normal(ks[5], (E, H, D), jnp.float32) * 0.02
        return {'x': x, 'Wr': Wr, 'br': br, 'Wgate': Wgate, 'bgate': bgate, 'W1': W1, 'W3': W3, 'W2': W2}
    _L0_ffn_all = _L0_ffn_setup()
    _L0_ffn_in = {k: v for k, v in _L0_ffn_all.items() if k in ('Wr', 'br', 'Wgate', 'bgate', 'W1', 'W3', 'W2')}
    del _L0_ffn_all
    return {'x': x, 'src': src, 'dst': dst, 'edge_weight': edge_weight, 'L0_gnn_W': _L0_gnn_in['W'], 'L0_gnn_bias': _L0_gnn_in['bias'], 'L0_ffn_Wr': _L0_ffn_in['Wr'], 'L0_ffn_br': _L0_ffn_in['br'], 'L0_ffn_Wgate': _L0_ffn_in['Wgate'], 'L0_ffn_bgate': _L0_ffn_in['bgate'], 'L0_ffn_W1': _L0_ffn_in['W1'], 'L0_ffn_W3': _L0_ffn_in['W3'], 'L0_ffn_W2': _L0_ffn_in['W2']}

def reference(x, src, dst, edge_weight, L0_gnn_W, L0_gnn_bias, L0_ffn_Wr, L0_ffn_br, L0_ffn_Wgate, L0_ffn_bgate, L0_ffn_W1, L0_ffn_W3, L0_ffn_W2):
    import jax
    import jax.numpy as jnp

    def _L0_gnn_ref(H, W, bias, edge_row, edge_col, edge_val):
        import jax, jax.numpy as jnp
        import numpy as np
        N_NODES = 1024
        HW = H @ W
        msgs = edge_val[:, None] * HW[edge_col]
        out = jax.ops.segment_sum(msgs, edge_row, num_segments=N_NODES)
        out = out + bias
        return jax.nn.relu(out)

    def _L0_ffn_ref(x, Wr, br, Wgate, bgate, W1, W3, W2):
        import jax, jax.numpy as jnp
        import numpy as np
        G = 4
        EPG = 4
        E = 16
        KG = 2
        K = 2
        GTP = 0.9
        TP = 0.9
        SCALE = 1.0 / float(np.sqrt(G))

        def _routing_weights(xf, Wr, br, Wgate, bgate):
            N = xf.shape[0]
            gp = jax.nn.softmax(xf @ Wr + br, axis=-1)
            order = jnp.argsort(-gp, axis=-1)
            sp_k = jnp.take_along_axis(gp, order, axis=-1)[:, :KG]
            idx_k = order[:, :KG]
            act = jnp.cumsum(sp_k, axis=-1) <= GTP
            act = act.at[:, 0].set(True)
            mp = sp_k * act
            rn = mp / (jnp.sum(mp, axis=-1, keepdims=True) + 1e-09)
            w_group = jnp.zeros((N, G), xf.dtype).at[jnp.arange(N)[:, None], idx_k].set(rn)
            ep = jax.nn.softmax(jnp.einsum('nd,gde->nge', xf, Wgate) + bgate, axis=-1)
            eorder = jnp.argsort(-ep, axis=-1)
            esp = jnp.take_along_axis(ep, eorder, axis=-1)[:, :, :K]
            eidx = eorder[:, :, :K]
            eact = jnp.cumsum(esp, axis=-1) <= TP
            eact = eact.at[:, :, 0].set(True)
            emp = esp * eact
            ern = emp / (jnp.sum(emp, axis=-1, keepdims=True) + 1e-09)
            w_exp = jnp.zeros((N, G, EPG), xf.dtype).at[jnp.arange(N)[:, None, None], jnp.arange(G)[None, :, None], eidx].set(ern)
            return (w_group[:, :, None] * w_exp * SCALE).reshape(N, E)
        B, T, D = x.shape
        xf = x.reshape(-1, D)
        tw = _routing_weights(xf, Wr, br, Wgate, bgate)
        out = jnp.zeros_like(xf)
        for e in range(E):
            h = jax.nn.silu(xf @ W1[e]) * (xf @ W3[e])
            out = out + tw[:, e:e + 1] * (h @ W2[e])
        return out.reshape(B, T, D)
    x = x + _L0_gnn_ref(_layernorm(x, axis=-1), L0_gnn_W, L0_gnn_bias, src, dst, edge_weight)
    x = x + _L0_ffn_ref(_layernorm(x, axis=-1)[None], L0_ffn_Wr, L0_ffn_br, L0_ffn_Wgate, L0_ffn_bgate, L0_ffn_W1, L0_ffn_W3, L0_ffn_W2)[0]
    return x

_drawn_inputs = setup_inputs


def setup_inputs(seed=0):
    import zlib

    import numpy as np

    out = dict(_drawn_inputs(seed))
    spreads = {'L0_gnn_bias': (0.0, 0.1), 'L0_ffn_br': (0.0, 0.8), 'L0_ffn_bgate': (0.0, 0.8)}
    factors = {'L0_ffn_Wr': 8.0,
     'L0_ffn_Wgate': 8.0,
     'L0_ffn_W1': 8.0,
     'L0_ffn_W3': 8.0,
     'L0_ffn_W2': 8.0}
    for name, (base, spread) in spreads.items():
        noise = np.random.default_rng([zlib.crc32(name.encode()), seed]).standard_normal(out[name].shape)
        drawn = base * np.exp(spread * noise) if base else spread * noise
        out[name] = jnp.asarray(drawn.astype(out[name].dtype))
    for name, factor in factors.items():
        out[name] = (out[name] * factor).astype(out[name].dtype)
    return out
```

```python
from contextlib import ExitStack

import concourse.bass as bass
from concourse import mybir

ALU = mybir.AluOpType
ACT = mybir.ActivationFunctionType
AX_X = mybir.AxisListType.X
F32 = mybir.dt.float32
F32R = mybir.dt.float32r
BF16 = mybir.dt.bfloat16
FP16 = mybir.dt.float16
I32 = mybir.dt.int32

P = 128
N = 1024
D = 512
NE = 16384
E = 16
G = 4
NT = N // P
HT = NT // 2
K = D // P
ET = NE // P
GRP = 2
NG = ET // GRP
SH = N // P
WIN = 40
WC = WIN * SH
BT = 8
BG = BT // GRP
QB = 4
BODIES = ET // (BT * QB)
BODYG = QB * BG
NC = N * SH
LAG = 2
HB = 4
AR = 6
EPS = 1e-5


def gnn_ffn(nc, x, src, dst, edge_weight, w_gnn, bias_gnn, w_r, b_r, w_gate, b_gate, w1, w3, w2, out):
    with ExitStack() as ctx:
        def sb(name, shape, dt):
            return ctx.enter_context(nc.sbuf_tensor(name, shape, dt))

        def sem(name):
            return ctx.enter_context(nc.semaphore(name))

        def region(name, size):
            slab = sb(name, [P, size // 4], F32)
            return nc.sbuf_base - size if nc.sbuf_base - size >= 0 else slab

        def at(name, shape, dt, offset):
            return nc.alloc_sbuf_tensor_at(name, shape, dt, offset=offset)

        KB = 1024
        adj_at = region("adj_region", 34048)
        adj = at("adj", [P, NC + WC], F32, adj_at)
        xTh = at("xTh", [P, 2, K, HT * P], F32R, adj_at)
        xTl = at("xTl", [P, 2, K, HT * P], F32R, adj_at + 16 * KB)
        aT_at = region("aT_region", 32 * KB)
        aTh = at("aTh", [P, NT, HT * P], F32R, aT_at)
        aTl = at("aTl", [P, NT, HT * P], F32R, aT_at + 16 * KB)
        wgh = at("wgh", [P, K, D], F32R, aT_at)
        wgl = at("wgl", [P, K, D], F32R, aT_at + 8 * KB)
        nTh = at("nTh", [P, 2, K, P], F32R, aT_at + 16 * KB)
        nTl = at("nTl", [P, 2, K, P], F32R, aT_at + 20 * KB)
        expf = at("expf", [E, 4, P], F32, aT_at + 24 * KB)
        src_i, dst_i, lo_i, hi_i, ew, lo_f, comb = (
            at(n, [P, P], dt, aT_at + 26 * KB + 512 * i) for i, (n, dt) in enumerate(
                [("src_i", I32), ("dst_i", I32), ("lo_i", I32), ("hi_i", I32), ("ew", F32), ("lo_f", F32), ("comb", F32)]))
        dst_g = at("dst_g", [NG, GRP * P], I32, aT_at + 30 * KB)
        gdiag = at("gdiag", [NG, 2, NG], F32, aT_at + 31 * KB)
        hist_at = region("hist_region", 24 * KB)
        statn = at("statn", [P, 2, 3, P, BT], BF16, hist_at)
        moving = at("moving", [P, 2 * BT, WC], BF16, hist_at + 12 * KB)
        xn1 = at("xn1", [P, 2, D], F32, hist_at)
        gTh = at("gTh", [P, K, HT * P], F32R, hist_at)
        gTl = at("gTl", [P, K, HT * P], F32R, hist_at + 8 * KB)
        relu_in = at("relu_in", [P, 2, D], F32, hist_at + 16 * KB)
        twTh = at("twTh", [E, HT * P], F32R, hist_at + 20 * KB)
        twTl = at("twTl", [E, HT * P], F32R, hist_at + 22 * KB)
        hw_at = region("hw_region", 32 * KB)
        hwh = at("hwh", [P, NT, D], F32R, hw_at)
        hwl = at("hwl", [P, NT, D], F32R, hw_at + 16 * KB)
        silu = at("silu", [P, 2, HT * P], F32, hw_at)
        hidden = at("hidden", [P, 2, HT * P], F32, hw_at + 4 * KB)
        gated = at("gated", [P, 2, HT * P], F32, hw_at + 8 * KB)
        y_sb = at("y_sb", [P, 2, D], F32, hw_at + 12 * KB)
        w2h = at("w2h", [P, K, D], F32R, hw_at + 16 * KB)
        w2l = at("w2l", [P, K, D], F32R, hw_at + 24 * KB)
        st_at = region("stage_region", 16 * KB)
        stage = [at(f"stage{i}", [P, K * D], F32, st_at + 8 * KB * i) for i in range(2)]
        xn2 = at("xn2", [P, HT, D], F32, st_at)

        x_sb = sb("x_sb", [P, NT, D], F32)
        w1h, w1l, w3h, w3l = (sb(n, [P, K, D], F32R) for n in ("w1h", "w1l", "w3h", "w3l"))
        wrg_raw = sb("wrg_raw", [P, 5, K, G], F32)
        wrgh, wrgl = (sb(n, [P, K, 5 * G], F32R) for n in ("wrgh", "wrgl"))
        brg = sb("brg", [P, 5 * G], F32)
        biasb = sb("biasb", [P, D], F32)
        ident = sb("ident", [P, P], F32)
        ones = sb("ones", [NG, P], F32)
        epsb = sb("epsb", [P, 1], F32)
        iota_lo = sb("iota_lo", [P, P, BT], BF16)
        iota_win = sb("iota_win", [P, WC], FP16)
        tie = sb("tie", [P, G, G], F32)
        expand = sb("expand", [E, 4, P], F32R)
        gmm = sb("gmm", [NG, 2], F32)
        base8 = sb("base8", [P, NG], F32)
        gmax_row = sb("gmax_row", [1, NG], F32)
        span = sb("span", [1, NG], F32)
        spanm = sb("spanm", [1, 1], F32)
        kwin = sb("kwin", [1, N // WIN + 1], F32)
        kcmp = sb("kcmp", [1, N // WIN + 1], F32)
        nwin = sb("nwin", [1, 1], F32)
        nbody = sb("nbody", [1, 1], I32)
        offs = sb("offs", [1, NG], I32)
        combrel = sb("combrel", [P, ET], F32)
        src_lo = sb("src_lo", [P, ET], BF16)
        w_res = sb("w_res", [P, 3, ET], F32)
        w_parts = sb("w_parts", [P, 3, ET], BF16)
        onehot = sb("onehot", [P, P, BT], BF16)
        cur = sb("cur", [P, 2, BT], F32)
        stats = sb("stats", [P, NT, 6], F32)
        mv = sb("mv", [P, NT, 2], F32)
        std = sb("std", [P, NT], F32)
        rstd = sb("rstd", [P, NT], F32)
        NGR = HT * 5
        lg = sb("lg", [P, NGR, G], F32)
        gm = sb("gm", [P, NGR], F32)
        gc = sb("gc", [P, NGR, G], F32)
        ge = sb("ge", [P, NGR, G], F32)
        gs = sb("gs", [P, NGR], F32)
        gr = sb("gr", [P, NGR], F32)
        gp = sb("gp", [P, NGR, G], F32)
        gt = sb("gt", [P, NGR, G, G], F32)
        eq = sb("eq", [P, NGR, G, G], F32)
        rank = sb("rank", [P, NGR, G], F32)
        m2 = sb("m2", [P, NGR, G], F32)
        p2 = sb("p2", [P, NGR, G], F32)
        tw = sb("tw", [P, HT, E], F32)

        bank = [ctx.enter_context(nc.psum_tensor(f"bank{i}", [P, 512], F32)) for i in range(8)]

        names = """d_dstg d_edges d_wg d_w1 d_w3 d_w2 d_small
                   c_ident0 c_ident c_ones c_iota c_adj c_tie0 c_tie c_exp0 c_exp1 c_exp c_expand c_kwin
                   prep gdiag_done tr_ready tr_hi tr_done wg_hi wg_lo std_req std_done xn_done
                   hw_ready hw_hi hw_done split_hi split_lo nbody_done
                   onehot_done stat_done cur_done mov_ready grp_done add_done
                   acc_ready acc_free cb_done chain exp_req exp_done xn2_done
                   tw_done silu_done gated_done g_hi g_lo y_done"""
        S = {n: sem(n) for n in names.split()}
        d_x = [sem(f"d_x{t}") for t in range(NT)]

        d_out = [sem(f"d_out{i}") for i in range(2)]

        T = ["edges", "base"] + [("x", t) for t in range(NT)]
        T += [("a", 0, 0), ("a", 1, 0)]
        for cb in range(NT):
            if cb + 2 < NT:
                T.append(("a", cb + 2, 0))
            T.append(("a", cb, 1))
        for h in range(2):
            T += [("n", t) for t in range(h * HT, h * HT + HT)] + [("logits", h), ("tw", h)]
        HI = [u for u in T if u[0] in ("x", "a", "n", "tw")]
        A = [("gnn", t) for t in range(NT)]

        def ffn_uses(h, at_y=None):
            u = [("h1", h, 0), ("h3", h, 0)]
            if h:
                u += [("y", t) for t in range(HT)]
            u += [("h1", h, 1), ("h3", h, 1), ("tw", h, 0), ("tw", h, 1)]
            for j in (2, 3):
                u += [("h1", h, j), ("h3", h, j), ("tw", h, j)]
            return u

        A += ffn_uses(0) + ffn_uses(1) + [("y", t) for t in range(HT, NT)]

        def tbank(u):
            return bank[T.index(u) % 2]

        def abank(u):
            return bank[2 + A.index(u) % AR]

        block = ctx.enter_context(nc.Block())

        @block.sync
        def _(sp):
            sp.dma_start(dst_g[:, :], dst.rearrange("(g e) -> g e", g=NG)).then_inc(S["d_dstg"], 16)
            sp.dma_start(src_i[:, :], src.rearrange("(t e) -> t e", t=ET)).then_inc(S["d_edges"], 16)
            sp.dma_start(dst_i[:, :], dst.rearrange("(t e) -> t e", t=ET)).then_inc(S["d_edges"], 16)
            sp.dma_start(ew[:, :], edge_weight.rearrange("(t e) -> t e", t=ET)).then_inc(S["d_edges"], 16)
            for t in range(NT):
                sp.dma_start(x_sb[:, t, :], x[t * P:(t + 1) * P, :]).then_inc(d_x[t], 16)
            sp.dma_start(stage[1][:, :].rearrange("p (e a) -> p e a", e=E),
                         w1.rearrange("e (p k) h -> p e (k h)", k=K)).then_inc(S["d_w1"], 16)
            sp.wait_ge(S["wg_lo"], 1)
            sp.dma_start(stage[0][:, :].rearrange("p (e a) -> p e a", e=E),
                         w3.rearrange("e (p k) h -> p e (k h)", k=K)).then_inc(S["d_w3"], 16)
            sp.wait_ge(S["split_lo"], K)
            sp.dma_start(stage[1][:, :].rearrange("p (j n) -> p j n", j=K),
                         w2.rearrange("e h n -> (e h) n").rearrange("(j p) n -> p j n", p=P)).then_inc(S["d_w2"], 16)
            for t in range(NT):
                sp.wait_ge(S["y_done"], t + 1)
                sp.dma_start(out[t * P:(t + 1) * P, :], y_sb[:, t % 2, :]).then_inc(d_out[t % 2], 16)
            for i in range(2):
                sp.wait_ge(d_out[i], 16 * HT)

        @block.gpsimd
        def _(g):
            g.memset(ident[:, :], 0.0).then_inc(S["c_ident0"], 1)
            g.memset(ones[:, :], 1.0).then_inc(S["c_ones"], 1)
            g.memset(epsb[:, :], EPS).then_inc(S["c_ones"], 1)
            g.wait_ge(S["c_ident0"], 1)
            g.affine_select(out=ident[:, :], in_=ident[:, :], compare_op=ALU.not_equal, fill=1.0, base=0,
                            pattern=[[-1, P]], channel_multiplier=1).then_inc(S["c_ident"], 1)
            g.iota(kwin[:, :], pattern=[[WIN, N // WIN + 1]], base=0, channel_multiplier=0,
                   allow_small_or_imprecise_dtypes=True).then_inc(S["c_kwin"], 1)
            g.iota(iota_lo[:, :, :], pattern=[[1, P], [0, BT]], base=0, channel_multiplier=0,
                   allow_small_or_imprecise_dtypes=True).then_inc(S["c_iota"], 1)
            g.iota(iota_win[:, :], pattern=[[1, WC]], base=0, channel_multiplier=0,
                   allow_small_or_imprecise_dtypes=True).then_inc(S["c_iota"], 1)
            g.memset(adj[:, :], 0.0).then_inc(S["c_adj"], 1)
            g.memset(tie[:, :, :], 1.0).then_inc(S["c_tie0"], 1)
            g.wait_ge(S["c_tie0"], 1)
            g.affine_select(out=tie[:, :, :], in_=tie[:, :, :], compare_op=ALU.is_gt, fill=0.0, base=0,
                            pattern=[[1, G], [-1, G]], channel_multiplier=0).then_inc(S["c_tie"], 1)
            g.memset(expf[:, :, :], 1.0).then_inc(S["c_exp0"], 1)
            g.wait_ge(S["c_exp0"], 1)
            g.affine_select(out=expf[:, :, :], in_=expf[:, :, :], compare_op=ALU.is_ge, fill=0.0, base=0,
                            pattern=[[P, 4], [1, P]], channel_multiplier=-32).then_inc(S["c_exp1"], 1)
            g.wait_ge(S["c_exp1"], 1)
            g.affine_select(out=expf[:, :, :], in_=expf[:, :, :], compare_op=ALU.is_ge, fill=0.0, base=31,
                            pattern=[[-P, 4], [-1, P]], channel_multiplier=32).then_inc(S["c_exp"], 1)
            g.wait_ge(S["c_exp"], 1)
            g.tensor_copy(expand[:, :, :], expf[:, :, :]).then_inc(S["c_expand"], 1)
            g.wait_ge(S["d_small"], 16 * 11)
            raw = wrg_raw[:, :, :, :].rearrange("p s k e -> p k s e")
            n = 0
            for k in range(K):
                hi = wrgh[:, k, :].rearrange("p (s e) -> p s e", s=5)
                lo = wrgl[:, k, :].rearrange("p (s e) -> p s e", s=5)
                g.tensor_copy(hi, raw[:, k]).then_inc(S["split_hi"], 1)
                n += 1
                g.wait_ge(S["split_hi"], n)
                g.tensor_tensor(lo, raw[:, k], hi.bitcast(F32), ALU.subtract).then_inc(S["split_hi"], 1)
                n += 1
            for which, st, hi_t, lo_t in (("d_w1", 1, w1h, w1l), ("d_w3", 0, w3h, w3l), ("d_w2", 1, w2h, w2l)):
                g.wait_ge(S[which], 16)
                if which == "d_w2":
                    g.wait_ge(S["acc_ready"], NT)
                for k in range(K):
                    if which == "d_w2":
                        raw, hi, lo = stage[st][:, k * D:(k + 1) * D], hi_t[:, k, :], lo_t[:, k, :]
                    else:
                        raw = stage[st][:, :].rearrange("p (e k h) -> p k e h", e=E, k=K)[:, k]
                        hi = hi_t[:, k, :].rearrange("p (e h) -> p e h", e=E)
                        lo = lo_t[:, k, :].rearrange("p (e h) -> p e h", e=E)
                    g.tensor_copy(hi, raw).then_inc(S["split_hi"], 1)
                    n += 1
                    g.wait_ge(S["split_hi"], n)
                    g.tensor_tensor(lo, raw, hi.bitcast(F32), ALU.subtract).then_inc(S["split_lo"], 1)

        @block.scalar
        def _(act):
            act.dma_start(stage[0][:, :], w_gnn.rearrange("(p k) n -> p (k n)", k=K)).then_inc(S["d_wg"], 16)
            small = S["d_small"]
            act.dma_start(wrg_raw[:, 0, :, :], w_r.rearrange("(p k) e -> p k e", k=K)).then_inc(small, 16)
            for i in range(G):
                act.dma_start(wrg_raw[:, 1 + i, :, :], w_gate[i].rearrange("(p k) e -> p k e", k=K)).then_inc(small, 16)
            act.dma_start(brg[:, 0:G], b_r.rearrange("(a e) -> a e", a=1).broadcast_to([P, G])).then_inc(small, 16)
            for i in range(G):
                act.dma_start(brg[:, G + G * i:2 * G + G * i], b_gate[i:i + 1, :].broadcast_to([P, G])).then_inc(small, 16)
            act.dma_start(biasb[:, :], bias_gnn.rearrange("(a n) -> a n", a=1).broadcast_to([P, D])).then_inc(small, 16)

            def round_hi(use, dst_hi, src_psum):
                act.wait_ge(S["tr_ready"], T.index(use) + 1)
                act.copy(dst_hi, src_psum).then_inc(S["tr_hi"], 1)

            def roots(i):
                act.wait_ge(S["std_req"], i + 1)
                act.activation(std[:, i % 2 * HT:i % 2 * HT + HT], mv[:, i % 2 * HT:i % 2 * HT + HT, 1], ACT.Sqrt,
                               bias=epsb[:, 0:1]).then_inc(S["std_done"], 1)

            act.wait_ge(S["c_ones"], 2)
            act.wait_ge(S["d_wg"], 16)
            act.copy(wgh[:, :, :].rearrange("p k n -> p (k n)"), stage[0][:, :]).then_inc(S["wg_hi"], 1)
            roots(0)
            for t in range(NT):
                if t == 1:
                    roots(1)
                if t >= 2:
                    act.wait_ge(S["hw_ready"], t - 1)
                round_hi(("x", t), nTh[:, t % 2, :, :], tbank(("x", t))[:, :].rearrange("p (k r) -> p k r", k=K))
                if t >= 1:
                    act.wait_ge(S["hw_ready"], t)
                    act.copy(hwh[:, t - 1, :], bank[6 + (t - 1) % 2][:, :]).then_inc(S["hw_hi"], 1)
            act.wait_ge(S["hw_ready"], NT)
            act.copy(hwh[:, NT - 1, :], bank[6 + (NT - 1) % 2][:, :]).then_inc(S["hw_hi"], 1)
            act.wait_ge(S["c_expand"], 1)
            for u in T:
                if u[0] == "a":
                    if u[2] == 1:
                        act.wait_ge(S["cb_done"], u[1] + 1)
                    round_hi(u, aTh[:, u[1], :], tbank(u)[:, :])
            roots(2)
            for h in range(2):
                for t in range(h * HT, h * HT + HT):
                    round_hi(("n", t), xTh[:, h, :, (t % HT) * P:(t % HT + 1) * P],
                             tbank(("n", t))[:, :].rearrange("p (k r) -> p k r", k=K))
                act.wait_ge(S["exp_req"], h + 1)
                act.activation(ge[:, :, :], gc[:, :, :], ACT.Exp).then_inc(S["exp_done"], 1)

                def gate(j):
                    n = h * 4 + j
                    act.wait_ge(S["acc_ready"], A.index(("h1", h, j)) + 1)
                    if n >= 2:
                        act.wait_ge(S["acc_free"], A.index(("h3", *divmod(n - 2, 4))) + 1)
                    act.activation(silu[:, n % 2, :], abank(("h1", h, j))[:, :], ACT.Silu).then_inc(S["silu_done"], 1)

                def g_round(j):
                    n = h * 4 + j
                    act.wait_ge(S["gated_done"], n + 1)
                    act.copy(gTh[:, j, :], gated[:, n % 2, :]).then_inc(S["g_hi"], 1)

                gate(0)
                gate(1)
                round_hi(("tw", h), twTh[:, :], tbank(("tw", h))[0:E, :])
                g_round(0)
                g_round(1)
                if h == 0:
                    roots(3)
                for j in (2, 3):
                    gate(j)
                    g_round(j)

        @block.tensor
        def _(pe):
            used = [0, 0]

            def t_begin(use):
                assert T[used[0]] == use
                if used[0] >= 2:
                    pe.wait_ge(S["tr_done"], used[0] - 1)
                used[0] += 1
                return tbank(use)

            def a_begin(use):
                assert A[used[1]] == use, (A[used[1]], use)
                if used[1] >= AR:
                    pe.wait_ge(S["acc_free"], used[1] - AR + 1)
                used[1] += 1
                return abank(use)

            def split_product(out_ap, pairs):
                n, last = 0, 3 * len(pairs) - 1
                for lh, ll, rh, rl in pairs:
                    for a, b in ((lh, rh), (ll, rh), (lh, rl)):
                        ins = pe.matmul(out_ap, a, b, start=n == 0, stop=n == last)
                        n += 1
                return ins

            pe.wait_ge(S["c_ident"], 1)
            pe.wait_ge(S["d_edges"], 48)
            pe.wait_ge(S["prep"], 4)
            b = t_begin("edges")
            pe.transpose(b[:, 0:P], lo_f[:, :], ident[:, :])
            pe.transpose(b[:, P:2 * P], comb[:, :], ident[:, :])
            pe.transpose(b[:, 2 * P:3 * P], ew[:, :], ident[:, :]).then_inc(S["tr_ready"], 1)
            b = t_begin("base")
            pe.wait_ge(S["c_ones"], 2)
            pe.wait_ge(S["gdiag_done"], 2)
            pe.matmul(b[:, 0:2 * NG], ones[:, :], gdiag[:, :, :].rearrange("p s g -> p (s g)"),
                      start=True, stop=True).then_inc(S["tr_ready"], 1)

            def x_transposes(t):
                b = t_begin(("x", t))
                pe.wait_ge(S["xn_done"], t + 1)
                v = xn1[:, t % 2, :].rearrange("r (p k) -> r k p", k=K)
                for k in range(K):
                    ins = pe.transpose(b[:, k * P:(k + 1) * P], v[:, k], ident[:, :])
                ins.then_inc(S["tr_ready"], 1)

            x_transposes(0)
            pe.wait_ge(S["wg_lo"], 1)
            for t in range(NT):
                if t + 1 < NT:
                    x_transposes(t + 1)
                pe.wait_ge(S["tr_done"], T.index(("x", t)) + 1)
                if t >= 2:
                    pe.wait_ge(S["hw_done"], t - 1)
                split_product(bank[6 + t % 2][:, :],
                              [(nTh[:, t % 2, k, :], nTl[:, t % 2, k, :], wgh[:, k, :], wgl[:, k, :])
                               for k in range(K)]).then_inc(S["hw_ready"], 1)

            pe.wait_ge(S["nbody_done"], 1)
            bodies = pe.value_load(nbody[0:1, 0:1], min_val=BODIES, max_val=BODIES * (N // WIN + 1))
            with pe.Fori(0, bodies) as n:
                for gi in range(BODYG):
                    q, k = divmod(gi, BG)
                    if k == 0:
                        pe.wait_ge(S["stat_done"], n * QB + (q + 1))
                    pe.wait_ge(S["mov_ready"], n * BODYG + (gi + 1))
                    if gi >= HB:
                        pe.wait_ge(S["add_done"], n * BODYG + (gi - HB + 1))
                    m = 0
                    for i in range(GRP):
                        for part in range(3):
                            t = GRP * k + i
                            ins = pe.matmul(bank[2 + gi % HB][:, 0:WC], statn[:, q % 2, part, :, t],
                                            moving[:, q % 2 * BT + t, :], start=m == 0, stop=m == 3 * GRP - 1)
                            m += 1
                    ins.then_inc(S["grp_done"], 1)

            def a_transposes(use):
                _, cb, h = use
                b = t_begin(use)
                v = adj[:, cb * P * SH:(cb + 1) * P * SH].rearrange("r (c s) -> r s c", s=SH)
                for s in range(HT):
                    ins = pe.transpose(b[:, s * P:(s + 1) * P], v[:, h * HT + s], ident[:, :])
                ins.then_inc(S["tr_ready"], 1)

            def gnn_step(t, cb, first, last):
                s = t % HT
                m = 0
                for a, bb in ((aTh, hwh), (aTl, hwh), (aTh, hwl)):
                    ins = pe.matmul(abank(("gnn", t))[:, :], a[:, cb, s * P:(s + 1) * P], bb[:, cb, :],
                                    start=first and m == 0, stop=last and m == 2)
                    m += 1
                return ins

            pe.wait_ge(S["hw_done"], NT)
            pe.wait_ge(S["nbody_done"], 2)
            a_transposes(("a", 0, 0))
            a_transposes(("a", 1, 0))
            for t in range(HT):
                a_begin(("gnn", t))
            for cb in range(NT):
                pe.wait_ge(S["tr_done"], T.index(("a", cb, 0)) + 1)
                for t in range(HT):
                    ins = gnn_step(t, cb, cb == 0, cb == NT - 1)
                    if cb == NT - 1:
                        ins.then_inc(S["acc_ready"], 1)
                        if t == HT - 1:
                            pe.nop().then_inc(S["cb_done"], 1)
                    elif t == HT - 1:
                        ins.then_inc(S["cb_done"], 1)
                if cb + 2 < NT:
                    a_transposes(("a", cb + 2, 0))
                a_transposes(("a", cb, 1))

            def n_transposes(t):
                b = t_begin(("n", t))
                pe.wait_ge(S["xn2_done"], t + 1)
                v = xn2[:, t % HT, :].rearrange("r (p k) -> r k p", k=K)
                for k in range(K):
                    ins = pe.transpose(b[:, k * P:(k + 1) * P], v[:, k], ident[:, :])
                ins.then_inc(S["tr_ready"], 1)

            for t in range(HT, NT):
                a_begin(("gnn", t))
                for cb in range(NT):
                    if t == HT:
                        pe.wait_ge(S["tr_done"], T.index(("a", cb, 1)) + 1)
                    ins = gnn_step(t, cb, cb == 0, cb == NT - 1)
                ins.then_inc(S["acc_ready"], 1)
                if t == HT + 1:
                    n_transposes(0)
                    n_transposes(1)
                if t == HT + 2:
                    n_transposes(2)
                    n_transposes(3)

            def logits(h):
                b = t_begin(("logits", h))
                if h == 0:
                    pe.wait_ge(S["split_hi"], 2 * K)
                pe.wait_ge(S["tr_done"], T.index(("n", h * HT + HT - 1)) + 1)
                for s in range(HT):
                    r = slice(s * P, (s + 1) * P)
                    ins = split_product(b[:, s * 32:s * 32 + 5 * G],
                                        [(xTh[:, h, k, r], xTl[:, h, k, r], wrgh[:, k, :], wrgl[:, k, :])
                                         for k in range(K)])
                ins.then_inc(S["tr_ready"], 1)

            def hidden_product(h, j):
                for name, wh, wl in (("h1", w1h, w1l), ("h3", w3h, w3l)):
                    b = a_begin((name, h, j))
                    c = slice(j * P, (j + 1) * P)
                    split_product(b[:, :], [(wh[:, k, c], wl[:, k, c], xTh[:, h, k, :], xTl[:, h, k, :])
                                            for k in range(K)]).then_inc(S["acc_ready"], 1)

            def tw_transposes(h):
                b = t_begin(("tw", h))
                pe.wait_ge(S["tw_done"], HT * (h + 1))
                for s in range(HT):
                    ins = pe.transpose(b[0:E, s * P:(s + 1) * P], tw[:, s, :], ident[:, :])
                ins.then_inc(S["tr_ready"], 1)

            def tw_rows(h, j):
                b = a_begin(("tw", h, j))
                if j == 0:
                    pe.wait_ge(S["tr_done"], T.index(("tw", h)) + 1)
                pe.matmul(b[:, :], expand[:, j, :], twTh[:, :], start=True, stop=False)
                pe.matmul(b[:, :], expand[:, j, :], twTl[:, :], start=False, stop=True).then_inc(S["acc_ready"], 1)

            def output(h):
                pe.wait_ge(S["g_lo"], h * 4 + 4)
                if h == 0:
                    pe.wait_ge(S["split_lo"], 3 * K)
                for t in range(h * HT, h * HT + HT):
                    b = a_begin(("y", t))
                    r = slice(t % HT * P, (t % HT + 1) * P)
                    split_product(b[:, :], [(gTh[:, j, r], gTl[:, j, r], w2h[:, j, :], w2l[:, j, :])
                                            for j in range(K)]).then_inc(S["acc_ready"], 1)

            logits(0)
            pe.wait_ge(S["split_lo"], 2 * K)
            pe.wait_ge(S["c_expand"], 1)
            for h in range(2):
                hidden_product(h, 0)
                if h:
                    output(0)
                hidden_product(h, 1)
                tw_transposes(h)
                tw_rows(h, 0)
                tw_rows(h, 1)
                for j in (2, 3):
                    hidden_product(h, j)
                    tw_rows(h, j)
                if h == 0:
                    for t in range(HT, NT):
                        n_transposes(t)
                    logits(1)
            output(1)

        @block.vector
        def _(v):
            step = [0]

            def link(ins):
                step[0] += 1
                ins.then_inc(S["chain"], 1)
                v.wait_ge(S["chain"], step[0])

            v.wait_ge(S["d_edges"], 48)
            v.tensor_scalar(lo_i[:, :], src_i[:, :], P - 1, None, ALU.bitwise_and).then_inc(S["prep"], 1)
            v.tensor_scalar(hi_i[:, :], src_i[:, :], 7, None, ALU.logical_shift_right).then_inc(S["prep"], 1)
            v.wait_ge(S["prep"], 2)
            v.tensor_copy(lo_f[:, :], lo_i[:, :]).then_inc(S["prep"], 1)
            v.scalar_tensor_tensor(comb[:, :], dst_i[:, :], float(SH), hi_i[:, :], ALU.mult, ALU.add).then_inc(S["prep"], 1)
            v.wait_ge(S["d_dstg"], 16)
            v.tensor_reduce(gmm[:, 0:1], dst_g[:, :], AX_X, ALU.min)
            link(v.tensor_reduce(gmm[:, 1:2], dst_g[:, :], AX_X, ALU.max))
            v.wait_ge(S["c_ident"], 1)
            for s in range(2):
                v.tensor_scalar(gdiag[:, s, :], ident[0:NG, 0:NG], gmm[:, s:s + 1], None, ALU.mult).then_inc(S["gdiag_done"], 1)
            eb, bb = tbank("edges"), tbank("base")
            v.wait_ge(S["tr_ready"], 1)
            v.tensor_copy(src_lo[:, :], eb[:, 0:P])
            link(v.tensor_copy(w_res[:, 0, :], eb[:, 2 * P:3 * P]))
            link(v.tensor_copy(w_parts[:, 0, :], w_res[:, 0, :]))
            link(v.tensor_tensor(w_res[:, 1, :], w_res[:, 0, :], w_parts[:, 0, :], ALU.subtract))
            link(v.tensor_copy(w_parts[:, 1, :], w_res[:, 1, :]))
            link(v.tensor_tensor(w_res[:, 2, :], w_res[:, 1, :], w_parts[:, 1, :], ALU.subtract))
            v.tensor_copy(w_parts[:, 2, :], w_res[:, 2, :])
            v.wait_ge(S["tr_ready"], 2)
            v.tensor_copy(gmax_row[:, :], bb[0:1, NG:2 * NG])
            link(v.tensor_scalar(base8[:, :], bb[:, 0:NG], float(SH), None, ALU.mult))
            v.tensor_tensor(combrel[:, :].rearrange("p (g i) -> p g i", i=GRP),
                            eb[:, P:2 * P].rearrange("p (g i) -> p g i", i=GRP),
                            base8[:, :].unsqueeze(2).broadcast_to([P, NG, GRP]), ALU.subtract).then_inc(S["tr_done"], 1)
            v.tensor_copy(offs[:, :], base8[0:1, :])
            link(v.tensor_tensor(span[:, :], gmax_row[:, :], bb[0:1, 0:NG], ALU.subtract))
            v.engine_nop().then_inc(S["tr_done"], 1)
            link(v.tensor_reduce(spanm[:, :], span[:, :], AX_X, ALU.max))
            v.wait_ge(S["c_kwin"], 1)
            link(v.tensor_scalar(kcmp[:, :], kwin[:, :], spanm[:, 0:1], None, ALU.is_le))
            link(v.tensor_reduce(nwin[:, :], kcmp[:, :], AX_X, ALU.add))
            link(v.tensor_scalar(nbody[:, :], nwin[:, :], float(BODIES), None, ALU.mult))
            v.engine_nop().then_inc(S["nbody_done"], 1)

            v.wait_ge(S["wg_hi"], 1)
            v.tensor_tensor(wgl[:, :, :].rearrange("p k n -> p (k n)"), stage[0][:, :],
                            wgh[:, :, :].rearrange("p k n -> p (k n)").bitcast(F32), ALU.subtract).then_inc(S["wg_lo"], 1)

            def row_stats(t):
                v.bn_stats(stats[:, t, :], x_sb[:, t, :]).then_inc(S["chain"], 1)
                step[0] += 1
                v.wait_ge(S["chain"], step[0])
                return v.bn_aggr(mv[:, t, :], stats[:, t, :])

            def roots(i):
                v.wait_ge(S["std_done"], i + 1)
                h = slice(i % 2 * HT, i % 2 * HT + HT)
                link(v.reciprocal(rstd[:, h], std[:, h]))

            def tr_rest(use, dst_lo, src_psum, hi):
                v.wait_ge(S["tr_hi"], HI.index(use) + 1)
                return v.tensor_tensor(dst_lo, src_psum, hi.bitcast(F32), ALU.subtract).then_inc(S["tr_done"], 1)

            for i in range(2):
                for t in range(i * HT, i * HT + HT):
                    v.wait_ge(d_x[t], 16)
                    ins = row_stats(t)
                ins.then_inc(S["std_req"], 1)
            def normalize(t):
                if t % HT == 0:
                    roots(t // HT)
                if t >= 2:
                    v.wait_ge(S["tr_ready"], T.index(("x", t - 2)) + 1)
                v.tensor_scalar(xn1[:, t % 2, :], x_sb[:, t, :], mv[:, t, 0:1], rstd[:, t:t + 1],
                                ALU.subtract, ALU.mult).then_inc(S["xn_done"], 1)

            def hw_rest(t):
                v.wait_ge(S["hw_hi"], t + 1)
                v.tensor_tensor(hwl[:, t, :], bank[6 + t % 2][:, :], hwh[:, t, :].bitcast(F32),
                                ALU.subtract).then_inc(S["hw_done"], 1)

            normalize(0)
            for t in range(NT):
                if t + 1 < NT:
                    normalize(t + 1)
                if t >= 2:
                    v.wait_ge(S["hw_ready"], t - 1)
                tr_rest(("x", t), nTl[:, t % 2, :, :],
                        tbank(("x", t))[:, :].rearrange("p (k r) -> p k r", k=K), nTh[:, t % 2, :, :])
                if t >= 1:
                    hw_rest(t - 1)
            hw_rest(NT - 1)

            v.wait_ge(S["c_iota"], 2)
            v.wait_ge(S["c_adj"], 1)
            bodies = v.value_load(nbody[0:1, 0:1], min_val=BODIES, max_val=BODIES * (N // WIN + 1))
            with v.Fori(0, bodies) as n:
                b0 = v.snap(n & (BODIES - 1))
                columns = []

                def add(gi):
                    v.wait_ge(S["grp_done"], n * BODYG + (gi + 1))
                    if gi:
                        v.wait_ge(S["add_done"], n * BODYG + gi)
                    a = adj[:, bass.ds(columns[gi], WC)]
                    v.tensor_tensor(a, a, bank[2 + gi % HB][:, 0:WC], ALU.add).then_inc(S["add_done"], 1)

                for q in range(QB):
                    t0 = b0 * (BT * QB) + BT * q
                    v.tensor_tensor(onehot[:, :, :], iota_lo[:, :, :],
                                    src_lo[:, bass.ds(t0, BT)].unsqueeze(1).broadcast_to([P, P, BT]),
                                    ALU.is_equal).then_inc(S["onehot_done"], 1)
                    v.wait_ge(S["onehot_done"], n * QB + (q + 1))
                    v.tensor_tensor(statn[:, q % 2, :, :, :],
                                    onehot[:, :, :].unsqueeze(1).broadcast_to([P, 3, P, BT]),
                                    w_parts[:, :, bass.ds(t0, BT)].unsqueeze(2).broadcast_to([P, 3, P, BT]),
                                    ALU.mult).then_inc(S["stat_done"], 1)
                    og = offs[0:1, bass.ds(b0 * BODYG + BG * q, BG)]
                    columns += nc.values_load_multi_w_load_instructions(
                        og, engines=[mybir.EngineType.DVE], min_val=0, max_val=NC)[1]
                    v.tensor_scalar(og, og, float(WC), float(NC), ALU.add, ALU.min)
                    v.tensor_copy(cur[:, q % 2, :], combrel[:, bass.ds(t0, BT)]).then_inc(S["cur_done"], 1)
                    v.wait_ge(S["cur_done"], n * QB + (q + 1))
                    v.tensor_scalar(combrel[:, bass.ds(t0, BT)], cur[:, q % 2, :], float(-WC), None, ALU.add)
                    for k in range(BG):
                        gi = q * BG + k
                        for i in range(GRP):
                            t = GRP * k + i
                            ins = v.tensor_scalar(moving[:, q % 2 * BT + t, :], iota_win[:, :],
                                                  cur[:, q % 2, t:t + 1], None, ALU.is_equal)
                        ins.then_inc(S["mov_ready"], 1)
                        if gi >= LAG:
                            add(gi - LAG)
                for gi in range(BODYG - LAG, BODYG):
                    add(gi)
                v.wait_ge(S["add_done"], n * BODYG + BODYG)
            v.engine_nop().then_inc(S["nbody_done"], 1)

            for u in T:
                if u[0] == "a":
                    if u[2] == 1:
                        v.wait_ge(S["cb_done"], u[1] + 1)
                    tr_rest(u, aTl[:, u[1], :], tbank(u)[:, :], aTh[:, u[1], :])

            v.wait_ge(S["d_small"], 16 * 11)

            def gnn_out(t):
                v.wait_ge(S["acc_ready"], A.index(("gnn", t)) + 1)
                ins = v.tensor_tensor(relu_in[:, t % 2, :], abank(("gnn", t))[:, :], biasb[:, :], ALU.add)
                ins.then_inc(S["acc_free"], 1)
                v.wait_ge(S["acc_free"], t + 1)
                link(v.scalar_tensor_tensor(x_sb[:, t, :], relu_in[:, t % 2, :], 0.0, x_sb[:, t, :], ALU.max, ALU.add))
                ins = row_stats(t)
                if t % HT == HT - 1:
                    ins.then_inc(S["std_req"], 1)

            def normalize2(t):
                if t >= HT:
                    v.wait_ge(S["tr_ready"], T.index(("n", t - HT)) + 1)
                v.tensor_scalar(xn2[:, t % HT, :], x_sb[:, t, :], mv[:, t, 0:1], rstd[:, t:t + 1],
                                ALU.subtract, ALU.mult).then_inc(S["xn2_done"], 1)

            def n_rest(t):
                r = slice(t % HT * P, (t % HT + 1) * P)
                tr_rest(("n", t), xTl[:, t // HT, :, r], tbank(("n", t))[:, :].rearrange("p (k r) -> p k r", k=K),
                        xTh[:, t // HT, :, r])

            def routing(h):
                v.wait_ge(S["tr_ready"], T.index(("logits", h)) + 1)
                lb = tbank(("logits", h))[:, 0:HT * 32].rearrange("p (s a) -> p s a", s=HT)[:, :, 0:5 * G]
                v.tensor_tensor(lg[:, :, :].rearrange("p (s a) e -> p s (a e)", s=HT), lb,
                                brg[:, :].unsqueeze(1).broadcast_to([P, HT, 5 * G]), ALU.add).then_inc(S["tr_done"], 1)
                v.wait_ge(S["tr_done"], T.index(("logits", h)) + 1)

                def over(a):
                    return a[:, :].unsqueeze(2).broadcast_to([P, NGR, G])

                link(v.tensor_reduce(gm[:, :], lg[:, :, :], AX_X, ALU.max))
                v.tensor_tensor(gc[:, :, :], lg[:, :, :], over(gm), ALU.subtract).then_inc(S["exp_req"], 1)
                v.wait_ge(S["exp_done"], h + 1)
                link(v.tensor_reduce(gs[:, :], ge[:, :, :], AX_X, ALU.add))
                link(v.reciprocal(gr[:, :], gs[:, :]))
                link(v.tensor_tensor(gp[:, :, :], ge[:, :, :], over(gr), ALU.mult))
                pj = gp[:, :, :].unsqueeze(2).broadcast_to([P, NGR, G, G])
                pi = gp[:, :, :].unsqueeze(3).broadcast_to([P, NGR, G, G])
                v.tensor_tensor(gt[:, :, :, :], pj, pi, ALU.is_gt)
                link(v.tensor_tensor(eq[:, :, :, :], pj, pi, ALU.is_equal))
                link(v.tensor_tensor(eq[:, :, :, :].rearrange("p a i j -> p a (i j)"),
                                     eq[:, :, :, :].rearrange("p a i j -> p a (i j)"),
                                     tie[:, :, :].rearrange("p i j -> p (i j)").unsqueeze(1).broadcast_to([P, NGR, G * G]),
                                     ALU.mult))
                link(v.tensor_tensor(gt[:, :, :, :], gt[:, :, :, :], eq[:, :, :, :], ALU.add))
                link(v.tensor_reduce(rank[:, :, :], gt[:, :, :, :], AX_X, ALU.add))
                link(v.scalar_tensor_tensor(p2[:, :, :], rank[:, :, :], 1.0, gp[:, :, :], ALU.is_le, ALU.mult))
                link(v.tensor_reduce(gs[:, :], p2[:, :, :], AX_X, ALU.add))
                link(v.tensor_scalar(gr[:, :], gs[:, :], 0.9, None, ALU.is_le))
                link(v.tensor_tensor(m2[:, :, :], rank[:, :, :], over(gr), ALU.is_le))
                link(v.tensor_tensor(p2[:, :, :], gp[:, :, :], m2[:, :, :], ALU.mult))
                link(v.tensor_reduce(gs[:, :], p2[:, :, :], AX_X, ALU.add))
                link(v.tensor_scalar(gs[:, :], gs[:, :], 1e-9, None, ALU.add))
                link(v.reciprocal(gr[:, :], gs[:, :]))
                link(v.tensor_tensor(p2[:, :, :], p2[:, :, :], over(gr), ALU.mult))
                w5 = p2[:, :, :].rearrange("p (s a) e -> p s a e", s=HT)
                for s in range(HT):
                    wg = w5[:, s, 0, :].unsqueeze(2).broadcast_to([P, G, G])
                    v.scalar_tensor_tensor(tw[:, s, :].rearrange("p (g e) -> p g e", g=G), w5[:, s, 1:5, :],
                                                 0.5, wg, ALU.mult, ALU.mult).then_inc(S["tw_done"], 1)

            def hide(h, j):
                n = h * 4 + j
                u = A.index(("h3", h, j))
                v.wait_ge(S["silu_done"], n + 1)
                v.wait_ge(S["acc_ready"], u + 1)
                v.tensor_tensor(hidden[:, n % 2, :], silu[:, n % 2, :], abank(("h3", h, j))[:, :],
                                ALU.mult).then_inc(S["acc_free"], 2)

            def gate(h, j):
                n = h * 4 + j
                u = A.index(("tw", h, j))
                v.wait_ge(S["acc_ready"], u + 1)
                v.wait_ge(S["acc_free"], A.index(("h3", h, j)) + 1)
                if n >= 2:
                    v.wait_ge(S["g_hi"], n - 1)
                v.tensor_tensor(gated[:, n % 2, :], hidden[:, n % 2, :], abank(("tw", h, j))[:, :],
                                ALU.mult).then_inc(S["acc_free"], 1)
                v.wait_ge(S["acc_free"], u + 1)
                v.engine_nop().then_inc(S["gated_done"], 1)

            def gate_rest(h, j):
                n = h * 4 + j
                v.wait_ge(S["g_hi"], n + 1)
                v.tensor_tensor(gTl[:, j, :], gated[:, n % 2, :], gTh[:, j, :].bitcast(F32),
                                ALU.subtract).then_inc(S["g_lo"], 1)

            def finish(t):
                u = A.index(("y", t))
                v.wait_ge(S["acc_ready"], u + 1)
                if t >= 2:
                    v.wait_ge(d_out[t % 2], 16 * (t // 2))
                v.tensor_tensor(y_sb[:, t % 2, :], abank(("y", t))[:, :], x_sb[:, t, :], ALU.add).then_inc(S["acc_free"], 1)
                v.wait_ge(S["acc_free"], u + 1)
                v.engine_nop().then_inc(S["y_done"], 1)

            for t in range(HT):
                gnn_out(t)
            roots(2)
            v.wait_ge(S["split_lo"], 2 * K)
            for t in range(HT):
                normalize2(t)
            n_rest(0)
            n_rest(1)
            gnn_out(HT)
            gnn_out(HT + 1)
            n_rest(2)
            n_rest(3)
            gnn_out(HT + 2)
            gnn_out(HT + 3)
            routing(0)
            for h in range(2):
                hide(h, 0)
                if h:
                    for t in range(HT):
                        finish(t)
                hide(h, 1)
                v.wait_ge(S["tr_hi"], HI.index(("tw", h)) + 1)
                v.tensor_tensor(twTl[:, :], tbank(("tw", h))[0:E, :], twTh[:, :].bitcast(F32),
                                ALU.subtract).then_inc(S["tr_done"], 1)
                gate(h, 0)
                gate(h, 1)
                gate_rest(h, 0)
                gate_rest(h, 1)
                if h == 0:
                    roots(3)
                    for t in range(HT, NT):
                        normalize2(t)
                for j in (2, 3):
                    hide(h, j)
                    gate(h, j)
                    gate_rest(h, j)
                if h == 0:
                    for t in range(HT, NT):
                        n_rest(t)
                    routing(1)
            for t in range(HT, NT):
                finish(t)


_INS = ["x", "src", "dst", "edge_weight", "L0_gnn_W", "L0_gnn_bias", "L0_ffn_Wr", "L0_ffn_br", "L0_ffn_Wgate",
        "L0_ffn_bgate", "L0_ffn_W1", "L0_ffn_W3", "L0_ffn_W2"]


def kernel(**inputs):
    import numpy as _np
    import concourse.bacc as _bacc
    from concourse import mybir as _mybir
    from concourse.bass_utils import run_bass_kernel_spmd as _run

    nc = _bacc.Bacc("TRN2", target_bir_lowering=False, num_devices=1)
    arrays, args = {}, []
    for name in _INS:
        a = _np.ascontiguousarray(inputs[name])
        arrays[f"in_{name}_dram"] = a
        args.append(nc.dram_tensor(f"in_{name}_dram", a.shape, _mybir.dt.from_np(a.dtype), kind="ExternalInput").ap())
    args.append(nc.dram_tensor("out_0_dram", (N, D), F32, kind="ExternalOutput").ap())
    gnn_ffn(nc, *args)
    r = _run(nc, [arrays], core_ids=[0])
    return r.results[0]["out_0_dram"]
```

```python
from contextlib import ExitStack

import concourse.bass as bass
from concourse import mybir

ALU = mybir.AluOpType
ACT = mybir.ActivationFunctionType
AX_X = mybir.AxisListType.X
F32 = mybir.dt.float32
F32R = mybir.dt.float32r
BF16 = mybir.dt.bfloat16
FP16 = mybir.dt.float16
I32 = mybir.dt.int32

P = 128
N = 1024
D = 512
NE = 16384
E = 16
G = 4
NT = N // P
HT = NT // 2
K = D // P
ET = NE // P
GRP = 2
NG = ET // GRP
SH = N // P
WIN = 36
WC = WIN * SH
BT = 8
BG = BT // GRP
NC = N * SH
NB = ET // BT
ROOTS = [(0, 2), (2, 4), (4, 8), (0, 4), (4, 8)]
LAG = 2
HB = 4
AR = 6
EPS = 1e-5


def gnn_ffn(nc, x, src, dst, edge_weight, w_gnn, bias_gnn, w_r, b_r, w_gate, b_gate, w1, w3, w2, out):
    with ExitStack() as ctx:
        def sb(name, shape, dt):
            return ctx.enter_context(nc.sbuf_tensor(name, shape, dt))

        def sem(name):
            return ctx.enter_context(nc.semaphore(name))

        def region(name, size):
            slab = sb(name, [P, size // 4], F32)
            return nc.sbuf_base - size if nc.sbuf_base - size >= 0 else slab

        def at(name, shape, dt, offset):
            return nc.alloc_sbuf_tensor_at(name, shape, dt, offset=offset)

        KB = 1024
        adj_at = region("adj_region", 34048)
        adj = at("adj", [P, NC + WC], F32, adj_at)
        xTh = at("xTh", [P, 2, K, HT * P], F32R, adj_at)
        xTl = at("xTl", [P, 2, K, HT * P], F32R, adj_at + 16 * KB)
        aT_at = region("aT_region", 32 * KB)
        aTh = at("aTh", [P, NT, HT * P], F32R, aT_at)
        aTl = at("aTl", [P, NT, HT * P], F32R, aT_at + 16 * KB)
        wgh = at("wgh", [P, K, D], F32R, aT_at)
        wgl = at("wgl", [P, K, D], F32R, aT_at + 8 * KB)
        nTh = at("nTh", [P, 2, K, P], F32R, aT_at + 16 * KB)
        nTl = at("nTl", [P, 2, K, P], F32R, aT_at + 20 * KB)
        expf = at("expf", [E, 4, P], F32, aT_at + 24 * KB)
        src_i, dst_i, lo_i, hi_i, ew, lo_f, comb = (
            at(n, [P, P], dt, aT_at + 26 * KB + 512 * i) for i, (n, dt) in enumerate(
                [("src_i", I32), ("dst_i", I32), ("lo_i", I32), ("hi_i", I32), ("ew", F32), ("lo_f", F32), ("comb", F32)]))
        raw = at("raw", [P, 2, D], F32, aT_at + 26 * KB)
        silu = at("silu", [P, K, HT * P], F32, aT_at)
        hidden = at("hidden", [P, K, HT * P], F32, aT_at + 8 * KB)
        gated = at("gated", [P, K, HT * P], F32, aT_at + 16 * KB)
        dst_g = at("dst_g", [NG, GRP * P], I32, aT_at + 30 * KB)
        gdiag = at("gdiag", [NG, 2, NG], F32, aT_at + 31 * KB)
        hist_at = region("hist_region", 24 * KB)
        statn = at("statn", [P, 3, 3, P, BT], BF16, hist_at)
        moving = at("moving", [P, BT, WC], BF16, hist_at + 18 * KB)
        gTh = at("gTh", [P, K, HT * P], F32R, hist_at)
        gTl = at("gTl", [P, K, HT * P], F32R, hist_at + 8 * KB)
        relu_in = at("relu_in", [P, 2, D], F32, hist_at + 16 * KB)
        twTh = at("twTh", [E, HT * P], F32R, hist_at + 20 * KB)
        twTl = at("twTl", [E, HT * P], F32R, hist_at + 22 * KB)
        hw_at = region("hw_region", 32 * KB)
        hwh = at("hwh", [P, NT, D], F32R, hw_at)
        hwl = at("hwl", [P, NT, D], F32R, hw_at + 16 * KB)
        y_sb = at("y_sb", [P, 4, D], F32, hw_at)
        lgT = at("lgT", [5 * G, HT * P], F32, hw_at + 8 * KB)
        w2h = at("w2h", [P, K, D], F32R, hw_at + 16 * KB)
        w2l = at("w2l", [P, K, D], F32R, hw_at + 24 * KB)
        w13_at = region("w13_region", 32 * KB)
        w1h, w1l, w3h, w3l = (at(n, [P, K, D], F32R, w13_at + 8 * KB * i)
                              for i, n in enumerate(("w1h", "w1l", "w3h", "w3l")))
        onehot = at("onehot", [P, ET // BT, P, BT], BF16, w13_at)
        st_at = region("stage_region", 16 * KB)
        stage = [at(f"stage{i}", [P, K * D], F32, st_at + 8 * KB * i) for i in range(2)]
        xn1 = at("xn1", [P, 2, D], F32, st_at + 8 * KB)
        xn2 = at("xn2", [P, HT, D], F32, st_at)

        x_sb = sb("x_sb", [P, NT, D], F32)
        wrg_raw = sb("wrg_raw", [P, 5, K, G], F32)
        wrgh, wrgl = (sb(n, [P, K, 5 * G], F32R) for n in ("wrgh", "wrgl"))
        brg = sb("brg", [P, 5 * G], F32)
        biasb = sb("biasb", [P, D], F32)
        ident = sb("ident", [P, P], F32)
        ones = sb("ones", [NG, P], F32)
        epsb = sb("epsb", [P, 1], F32)
        iota_lo = sb("iota_lo", [P, P, BT], BF16)
        iota_win = sb("iota_win", [P, WC], FP16)
        tie = sb("tie", [P, G, G], F32)
        expand = sb("expand", [E, 4, P], F32R)
        gmm = sb("gmm", [NG, 2], F32)
        base8 = sb("base8", [P, NG], F32)
        gmax_row = sb("gmax_row", [1, NG], F32)
        span = sb("span", [1, NG], F32)
        spanm = sb("spanm", [1, 1], F32)
        kwin = sb("kwin", [1, N // WIN + 1], F32)
        kcmp = sb("kcmp", [1, N // WIN + 1], F32)
        nwin = sb("nwin", [1, 1], F32)
        nbody = sb("nbody", [1, 1], I32)
        offs = sb("offs", [1, NG], I32)
        combrel = sb("combrel", [P, ET], F32)
        src_lo = sb("src_lo", [P, ET], BF16)
        w_res = sb("w_res", [P, 3, ET], F32)
        w_parts = sb("w_parts", [P, 2, ET], BF16)
        stats = sb("stats", [P, NT, 6], F32)
        mv = sb("mv", [P, NT, 2], F32)
        std = sb("std", [P, NT], F32)
        rstd = sb("rstd", [P, NT], F32)
        NGR = HT * 5
        lg = sb("lg", [P, NGR, G], F32)
        gm = sb("gm", [P, NGR], F32)
        gc = sb("gc", [P, NGR, G], F32)
        ge = sb("ge", [P, NGR, G], F32)
        gs = sb("gs", [P, NGR], F32)
        gr = sb("gr", [P, NGR], F32)
        gp = sb("gp", [P, NGR, G], F32)
        gt = sb("gt", [P, NGR, G, G], F32)
        eq = sb("eq", [P, NGR, G, G], F32)
        rank = sb("rank", [P, NGR, G], F32)
        m2 = sb("m2", [P, NGR, G], F32)
        p2 = sb("p2", [P, NGR, G], F32)
        tw = sb("tw", [P, HT, E], F32)

        bank = [ctx.enter_context(nc.psum_tensor(f"bank{i}", [P, 512], F32)) for i in range(8)]

        names = """d_dstg d_edges d_wg d_w1 d_w3 d_w2 d_small
                   c_ident0 c_ident c_ones c_iota c_adj c_tie0 c_tie c_exp0 c_exp1 c_exp c_expand c_kwin
                   prep gdiag_done tr_ready tr_hi tr_done raw_done raw_rest c_table wg_hi wg_lo std_req std_done xn_done
                   hw_ready split_hi split_lo nbody_done
                   onehot_done rel_done stat_done second_done rest_done cur_done mov_ready grp_done add_done
                   acc_ready acc_free cb_done chain lgT_done exp_req exp_done xn2_done
                   tw_done silu_done gated_done g_hi g_lo y_done"""
        S = {n: sem(n) for n in names.split()}
        d_x = [sem(f"d_x{t}") for t in range(NT)]

        d_out = [sem(f"d_out{i}") for i in range(4)]

        T = ["edges", "base"] + [("x", t) for t in range(NT)]
        T += [("a", 0, 0), ("a", 1, 0)]
        for cb in range(NT):
            if cb + 2 < NT:
                T.append(("a", cb + 2, 0))
            T.append(("a", cb, 1))
        for h in range(2):
            T += [("n", t) for t in range(h * HT, h * HT + HT)] + [("lgT", h), ("logits", h), ("tw", h)]
        HI = [u for u in T if u[0] in ("a", "n", "tw")]
        LO = [u for u in T if u[0] not in ("x", "lgT")]
        R = [("x", 0), ("x", 1)]
        for t in range(2, NT):
            R += [("hw", t - 2), ("x", t)]
        R += [("hw", NT - 2), ("hw", NT - 1)]
        A = [("gnn", t) for t in range(NT)]

        def ffn_uses(h):
            u = [("h1", h, 0), ("h3", h, 0)]
            if h:
                u += [("y", t) for t in range(HT)]
            u += [("h1", h, 1), ("h3", h, 1)]
            if h:
                u += [("tw", h, 0), ("tw", h, 1), ("h1", h, 2), ("h3", h, 2), ("tw", h, 2)]
            else:
                u += [("h1", h, 2), ("h3", h, 2), ("tw", h, 0), ("tw", h, 1), ("tw", h, 2)]
            return u + [("h1", h, 3), ("h3", h, 3), ("tw", h, 3)]

        A += ffn_uses(0) + ffn_uses(1) + [("y", t) for t in range(HT, NT)]

        def tbank(u):
            return bank[T.index(u) % 2]

        def abank(u):
            return bank[2 + A.index(u) % AR]

        block = ctx.enter_context(nc.Block())

        @block.sync
        def _(sp):
            sp.dma_start(dst_g[:, :], dst.rearrange("(g e) -> g e", g=NG)).then_inc(S["d_dstg"], 16)
            sp.dma_start(src_i[:, :], src.rearrange("(t e) -> t e", t=ET)).then_inc(S["d_edges"], 16)
            sp.dma_start(dst_i[:, :], dst.rearrange("(t e) -> t e", t=ET)).then_inc(S["d_edges"], 16)
            sp.dma_start(ew[:, :], edge_weight.rearrange("(t e) -> t e", t=ET)).then_inc(S["d_edges"], 16)
            for t in range(NT):
                sp.dma_start(x_sb[:, t, :], x[t * P:(t + 1) * P, :]).then_inc(d_x[t], 16)
                if t == 1:
                    sp.dma_start(stage[0][:, :], w_gnn.rearrange("(p k) n -> p (k n)", k=K)).then_inc(S["d_wg"], 16)
            small = S["d_small"]
            sp.dma_start(wrg_raw[:, 0, :, :], w_r.rearrange("(p k) e -> p k e", k=K)).then_inc(small, 16)
            sp.dma_start(wrg_raw[:, 1:1 + G, :, :].rearrange("p g k e -> p g (k e)"),
                         w_gate.rearrange("g (p k) e -> p g (k e)", k=K)).then_inc(small, 16)
            sp.dma_start(brg[:, 0:G], b_r.rearrange("(a e) -> a e", a=1).broadcast_to([P, G])).then_inc(small, 16)
            sp.dma_start(brg[:, G:5 * G], b_gate.rearrange("(a g) e -> a (g e)", a=1).broadcast_to([P, G * G]))\
              .then_inc(small, 16)
            sp.dma_start(biasb[:, :], bias_gnn.rearrange("(a n) -> a n", a=1).broadcast_to([P, D])).then_inc(small, 16)
            sp.wait_ge(S["wg_lo"], 1)
            sp.dma_start(stage[0][:, :].rearrange("p (e a) -> p e a", e=E),
                         w3.rearrange("e (p k) h -> p e (k h)", k=K)).then_inc(S["d_w3"], 16)
            sp.wait_ge(S["tr_ready"], T.index(("x", NT - 1)) + 1)
            sp.dma_start(stage[1][:, :].rearrange("p (e a) -> p e a", e=E),
                         w1.rearrange("e (p k) h -> p e (k h)", k=K)).then_inc(S["d_w1"], 16)
            sp.wait_ge(S["split_lo"], K)
            sp.dma_start(stage[1][:, :].rearrange("p (j n) -> p j n", j=K),
                         w2.rearrange("e h n -> (e h) n").rearrange("(j p) n -> p j n", p=P)).then_inc(S["d_w2"], 16)
            for t in range(NT):
                sp.wait_ge(S["y_done"], t + 1)
                sp.dma_start(out[t * P:(t + 1) * P, :], y_sb[:, t % 4, :]).then_inc(d_out[t % 4], 16)
            for i in range(4):
                sp.wait_ge(d_out[i], 16 * (NT // 4))

        @block.gpsimd
        def _(g):
            g.memset(ident[:, :], 0.0).then_inc(S["c_ident0"], 1)
            g.memset(ones[:, :], 1.0).then_inc(S["c_ones"], 1)
            g.memset(epsb[:, :], EPS).then_inc(S["c_ones"], 1)
            g.wait_ge(S["c_ident0"], 1)
            g.affine_select(out=ident[:, :], in_=ident[:, :], compare_op=ALU.not_equal, fill=1.0, base=0,
                            pattern=[[-1, P]], channel_multiplier=1).then_inc(S["c_ident"], 1)
            g.iota(kwin[:, :], pattern=[[WIN, N // WIN + 1]], base=0, channel_multiplier=0,
                   allow_small_or_imprecise_dtypes=True).then_inc(S["c_kwin"], 1)
            g.iota(iota_lo[:, :, :], pattern=[[1, P], [0, BT]], base=0, channel_multiplier=0,
                   allow_small_or_imprecise_dtypes=True).then_inc(S["c_iota"], 1)
            g.iota(iota_win[:, :], pattern=[[1, WC]], base=0, channel_multiplier=0,
                   allow_small_or_imprecise_dtypes=True).then_inc(S["c_iota"], 1)
            g.memset(adj[:, :], 0.0).then_inc(S["c_adj"], 1)
            g.wait_ge(S["wg_hi"], 1)
            g.tensor_tensor(wgl[:, :, :].rearrange("p k n -> p (k n)"), stage[0][:, :],
                            wgh[:, :, :].rearrange("p k n -> p (k n)").bitcast(F32), ALU.subtract).then_inc(S["wg_lo"], 1)

            def routing_constants():
                g.memset(tie[:, :, :], 1.0).then_inc(S["c_tie0"], 1)
                g.wait_ge(S["c_tie0"], 1)
                g.affine_select(out=tie[:, :, :], in_=tie[:, :, :], compare_op=ALU.is_gt, fill=0.0, base=0,
                                pattern=[[1, G], [-1, G]], channel_multiplier=0).then_inc(S["c_tie"], 1)
                g.memset(expf[:, :, :], 1.0).then_inc(S["c_exp0"], 1)
                g.wait_ge(S["c_exp0"], 1)
                g.affine_select(out=expf[:, :, :], in_=expf[:, :, :], compare_op=ALU.is_ge, fill=0.0, base=0,
                                pattern=[[P, 4], [1, P]], channel_multiplier=-32).then_inc(S["c_exp1"], 1)
                g.wait_ge(S["c_exp1"], 1)
                g.affine_select(out=expf[:, :, :], in_=expf[:, :, :], compare_op=ALU.is_ge, fill=0.0, base=31,
                                pattern=[[-P, 4], [-1, P]], channel_multiplier=32).then_inc(S["c_exp"], 1)
                g.wait_ge(S["c_exp"], 1)
                g.tensor_copy(expand[:, :, :], expf[:, :, :]).then_inc(S["c_expand"], 1)

            def rest_of(use):
                what, t = use
                m = R.index(use)
                g.wait_ge(S["raw_done"], m + 1)
                if what == "x":
                    hi, lo = nTh[:, t % 2, :, :].rearrange("p k r -> p (k r)"), nTl[:, t % 2, :, :].rearrange("p k r -> p (k r)")
                else:
                    hi, lo = hwh[:, t, :], hwl[:, t, :]
                g.tensor_tensor(lo, raw[:, m % 2, :], hi.bitcast(F32), ALU.subtract).then_inc(S["raw_rest"], 1)

            def sweep(n, first):
                for q in range(NB):
                    g.wait_ge(S["stat_done"], n * NB + (q + 1))
                    g.tensor_tensor(statn[:, q % 3, 1, :, :], onehot[:, q],
                                    w_parts[:, 1, q * BT:(q + 1) * BT].unsqueeze(1).broadcast_to([P, P, BT]),
                                    ALU.mult).then_inc(S["second_done"], 1)
                    t = q // 2 + 1
                    if first and q >= 2:
                        if q % 2 == 0:
                            rest_of(("hw", t - 2))
                        elif t < NT:
                            rest_of(("x", t))
                if first:
                    rest_of(("hw", NT - 1))

            rest_of(("x", 0))
            rest_of(("x", 1))
            sweep(0, True)
            g.wait_ge(S["nbody_done"], 1)
            sweeps = g.value_load(nbody[0:1, 0:1], min_val=1, max_val=N // WIN + 1)
            with g.If(sweeps > 1):
                with g.Fori(1, sweeps) as n:
                    sweep(n, False)
            routing_constants()
            g.wait_ge(S["d_small"], 16 * 5)
            wrg = wrg_raw[:, :, :, :].rearrange("p s k e -> p k s e")
            n = 0
            for k in range(K):
                hi = wrgh[:, k, :].rearrange("p (s e) -> p s e", s=5)
                lo = wrgl[:, k, :].rearrange("p (s e) -> p s e", s=5)
                g.tensor_copy(hi, wrg[:, k]).then_inc(S["split_hi"], 1)
                n += 1
                g.wait_ge(S["split_hi"], n)
                g.tensor_tensor(lo, wrg[:, k], hi.bitcast(F32), ALU.subtract).then_inc(S["split_hi"], 1)
                n += 1
            for which, st, hi_t, lo_t in (("d_w1", 1, w1h, w1l), ("d_w3", 0, w3h, w3l), ("d_w2", 1, w2h, w2l)):
                g.wait_ge(S[which], 16)
                if which == "d_w1":
                    g.wait_ge(S["nbody_done"], 2)
                    g.wait_ge(S["tr_hi"], HI.index(("a", 0, 0)) + 1)
                if which == "d_w2":
                    g.wait_ge(S["acc_ready"], NT)
                for k in range(K):
                    if which == "d_w2":
                        whole, hi, lo = stage[st][:, k * D:(k + 1) * D], hi_t[:, k, :], lo_t[:, k, :]
                    else:
                        whole = stage[st][:, :].rearrange("p (e k h) -> p k e h", e=E, k=K)[:, k]
                        hi = hi_t[:, k, :].rearrange("p (e h) -> p e h", e=E)
                        lo = lo_t[:, k, :].rearrange("p (e h) -> p e h", e=E)
                    g.tensor_copy(hi, whole).then_inc(S["split_hi"], 1)
                    n += 1
                    g.wait_ge(S["split_hi"], n)
                    g.tensor_tensor(lo, whole, hi.bitcast(F32), ALU.subtract).then_inc(S["split_lo"], 1)

        @block.scalar
        def _(act):
            def round_hi(use, dst_hi, src_psum):
                act.wait_ge(S["tr_ready"], T.index(use) + 1)
                act.copy(dst_hi, src_psum).then_inc(S["tr_hi"], 1)

            def roots(i):
                act.wait_ge(S["std_req"], i + 1)
                r = slice(*ROOTS[i])
                act.activation(std[:, r], mv[:, r, 1], ACT.Sqrt, bias=epsb[:, 0:1]).then_inc(S["std_done"], 1)

            act.wait_ge(S["c_ones"], 2)
            act.activation(std[:, 0:1], epsb[:, 0:1], ACT.Sqrt).then_inc(S["c_table"], 1)
            act.wait_ge(S["c_table"], 1)
            roots(0)
            act.wait_ge(S["d_wg"], 16)
            act.copy(wgh[:, :, :].rearrange("p k n -> p (k n)"), stage[0][:, :]).then_inc(S["wg_hi"], 1)

            def copy_and_round(use):
                what, t = use
                m = R.index(use)
                if what == "x":
                    act.wait_ge(S["tr_ready"], T.index(use) + 1)
                    if t >= 2:
                        act.wait_ge(S["hw_ready"], t - 1)
                    src_psum, hi = tbank(use)[:, :], nTh[:, t % 2, :, :].rearrange("p k r -> p (k r)")
                else:
                    act.wait_ge(S["hw_ready"], t + 1)
                    src_psum, hi = bank[6 + t % 2][:, :], hwh[:, t, :]
                act.copy(hi, src_psum)
                if m >= 2:
                    act.wait_ge(S["raw_rest"], m - 1)
                act.copy(raw[:, m % 2, :], src_psum).then_inc(S["raw_done"], 1)

            def third_parts(b, slot):
                for i in range(BT):
                    ins = act.activation(statn[:, slot, 2, :, i], onehot[:, b, :, i], ACT.Copy,
                                         scale=w_res[:, 2, b * BT + i:b * BT + i + 1])
                ins.then_inc(S["rest_done"], 1)

            def sweep(n, first):
                for q in range(NB):
                    act.wait_ge(S["stat_done"], n * NB + (q + 1))
                    third_parts(q, q % 3)
                    if first and q == 1:
                        roots(1)
                    if first and q == 4:
                        roots(2)
                    t = q // 2 + 1
                    if first and q >= 2:
                        if q % 2 == 0:
                            copy_and_round(("hw", t - 2))
                        elif t < NT:
                            copy_and_round(("x", t))
                if first:
                    copy_and_round(("hw", NT - 1))

            for use in R[:2]:
                copy_and_round(use)
            sweep(0, True)
            act.wait_ge(S["nbody_done"], 1)
            sweeps = act.value_load(nbody[0:1, 0:1], min_val=1, max_val=N // WIN + 1)
            with act.If(sweeps > 1):
                with act.Fori(1, sweeps) as n:
                    sweep(n, False)
            act.wait_ge(S["c_expand"], 1)
            for u in T:
                if u[0] == "a":
                    if u[2] == 1:
                        act.wait_ge(S["cb_done"], u[1] + 1)
                    round_hi(u, aTh[:, u[1], :], tbank(u)[:, :])
            def n_round(t):
                round_hi(("n", t), xTh[:, t // HT, :, (t % HT) * P:(t % HT + 1) * P],
                         tbank(("n", t))[:, :].rearrange("p (k r) -> p k r", k=K))

            def gate(n):
                h, j = divmod(n, K)
                act.wait_ge(S["acc_ready"], A.index(("h1", h, j)) + 1)
                if h:
                    act.wait_ge(S["acc_free"], A.index(("h3", 0, j)) + 1)
                act.activation(silu[:, j, :], abank(("h1", h, j))[:, :], ACT.Silu).then_inc(S["silu_done"], 1)

            def g_round(n):
                act.wait_ge(S["gated_done"], n + 1)
                act.copy(gTh[:, n % K, :], gated[:, n % K, :]).then_inc(S["g_hi"], 1)

            roots(3)
            for t in range(HT):
                n_round(t)
            for h in range(2):
                act.wait_ge(S["tr_ready"], T.index(("lgT", h)) + 1)
                act.copy(lgT[:, :], tbank(("lgT", h))[0:5 * G, :]).then_inc(S["lgT_done"], 1)
                act.wait_ge(S["exp_req"], h + 1)
                act.activation(ge[:, :, :], gc[:, :, :], ACT.Exp).then_inc(S["exp_done"], 1)
                for j in range(3 - h):
                    gate(K * h + j)
                if h == 0:
                    roots(4)
                round_hi(("tw", h), twTh[:, :], tbank(("tw", h))[0:E, :])
                g_round(K * h)
                if h == 0:
                    n_round(4)
                g_round(K * h + 1)
                if h == 0:
                    n_round(5)
                else:
                    gate(K + 2)
                g_round(K * h + 2)
                if h == 0:
                    n_round(6)
                    n_round(7)
                gate(K * h + 3)
                g_round(K * h + 3)

        @block.tensor
        def _(pe):
            used = [0, 0]

            def t_begin(use):
                assert T[used[0]] == use
                if used[0] >= 2:
                    before = T[used[0] - 2]
                    if before[0] == "x":
                        pe.wait_ge(S["raw_done"], R.index(before) + 1)
                    elif before[0] == "lgT":
                        pe.wait_ge(S["lgT_done"], before[1] + 1)
                    else:
                        pe.wait_ge(S["tr_done"], LO.index(before) + 1)
                used[0] += 1
                return tbank(use)

            def a_begin(use):
                assert A[used[1]] == use, (A[used[1]], use)
                if used[1] >= AR:
                    pe.wait_ge(S["acc_free"], used[1] - AR + 1)
                used[1] += 1
                return abank(use)

            def split_product(out_ap, pairs):
                n, last = 0, 3 * len(pairs) - 1
                for lh, ll, rh, rl in pairs:
                    for a, b in ((lh, rh), (ll, rh), (lh, rl)):
                        ins = pe.matmul(out_ap, a, b, start=n == 0, stop=n == last)
                        n += 1
                return ins

            pe.wait_ge(S["c_ident"], 1)
            pe.wait_ge(S["d_edges"], 48)
            pe.wait_ge(S["prep"], 4)
            b = t_begin("edges")
            pe.transpose(b[:, 0:P], lo_f[:, :], ident[:, :])
            pe.transpose(b[:, P:2 * P], comb[:, :], ident[:, :])
            pe.transpose(b[:, 2 * P:3 * P], ew[:, :], ident[:, :]).then_inc(S["tr_ready"], 1)
            b = t_begin("base")
            pe.wait_ge(S["c_ones"], 2)
            pe.wait_ge(S["gdiag_done"], 2)
            pe.matmul(b[:, 0:2 * NG], ones[:, :], gdiag[:, :, :].rearrange("p s g -> p (s g)"),
                      start=True, stop=True).then_inc(S["tr_ready"], 1)

            def x_transposes(t, k0):
                if k0 == 0:
                    t_begin(("x", t))
                    pe.wait_ge(S["xn_done"], t + 1)
                v = xn1[:, t % 2, :].rearrange("r (p k) -> r k p", k=K)
                for k in (k0, k0 + 1):
                    ins = pe.transpose(tbank(("x", t))[:, k * P:(k + 1) * P], v[:, k], ident[:, :])
                if k0 + 2 == K:
                    ins.then_inc(S["tr_ready"], 1)

            def x_product(t, sixth):
                if sixth == 0:
                    pe.wait_ge(S["raw_rest"], R.index(("x", t)) + 1)
                    if t >= 2:
                        pe.wait_ge(S["raw_done"], R.index(("hw", t - 2)) + 1)
                for m in (2 * sixth, 2 * sixth + 1):
                    k = m // 3
                    a, w = ((nTh, wgh), (nTl, wgh), (nTh, wgl))[m % 3]
                    ins = pe.matmul(bank[6 + t % 2][:, :], a[:, t % 2, k, :], w[:, k, :],
                                    start=m == 0, stop=m == 3 * K - 1)
                if sixth == 5:
                    ins.then_inc(S["hw_ready"], 1)

            def sweep(n, first):
                for g in range(NG):
                    q, k = divmod(g, BG)
                    if k == 0:
                        pe.wait_ge(S["stat_done"], n * NB + (q + 1))
                        pe.wait_ge(S["rest_done"], n * NB + (q + 1))
                        pe.wait_ge(S["second_done"], n * NB + (q + 1))
                    pe.wait_ge(S["mov_ready"], n * NG + (g + 1))
                    if g >= HB:
                        pe.wait_ge(S["add_done"], n * NG + (g - HB + 1))
                    m = 0
                    for i in range(GRP):
                        for part in range(3):
                            t = GRP * k + i
                            ins = pe.matmul(bank[2 + g % HB][:, 0:WC], statn[:, q % 3, part, :, t],
                                            moving[:, t, :], start=m == 0, stop=m == 3 * GRP - 1)
                            m += 1
                    ins.then_inc(S["grp_done"], 1)
                    if first and BG <= g < BG + 2 * BG * (NT - 1):
                        t, i = 1 + (g - BG) // (2 * BG), (g - BG) % (2 * BG)
                        if i in (2, 3):
                            if t + 1 < NT:
                                x_transposes(t + 1, (i - 2) * 2)
                        else:
                            i = i if i < 2 else i - 2
                            x_product(t, i)

            for t in range(2):
                x_transposes(t, 0)
                x_transposes(t, 2)
            pe.wait_ge(S["wg_lo"], 1)
            for sixth in range(6):
                x_product(0, sixth)
            sweep(0, True)
            pe.wait_ge(S["nbody_done"], 1)
            sweeps = pe.value_load(nbody[0:1, 0:1], min_val=1, max_val=N // WIN + 1)
            with pe.If(sweeps > 1):
                with pe.Fori(1, sweeps) as n:
                    sweep(n, False)

            def a_transposes(use):
                _, cb, h = use
                b = t_begin(use)
                v = adj[:, cb * P * SH:(cb + 1) * P * SH].rearrange("r (c s) -> r s c", s=SH)
                for s in range(HT):
                    ins = pe.transpose(b[:, s * P:(s + 1) * P], v[:, h * HT + s], ident[:, :])
                ins.then_inc(S["tr_ready"], 1)

            def gnn_step(t, cb, first, last):
                s = t % HT
                m = 0
                for a, bb in ((aTh, hwh), (aTl, hwh), (aTh, hwl)):
                    ins = pe.matmul(abank(("gnn", t))[:, :], a[:, cb, s * P:(s + 1) * P], bb[:, cb, :],
                                    start=first and m == 0, stop=last and m == 2)
                    m += 1
                return ins

            pe.wait_ge(S["raw_rest"], len(R))
            pe.wait_ge(S["nbody_done"], 2)
            a_transposes(("a", 0, 0))
            a_transposes(("a", 1, 0))
            for t in range(HT):
                a_begin(("gnn", t))
            for cb in range(NT):
                pe.wait_ge(S["tr_done"], LO.index(("a", cb, 0)) + 1)
                for t in range(HT):
                    ins = gnn_step(t, cb, cb == 0, cb == NT - 1)
                    if cb == NT - 1:
                        ins.then_inc(S["acc_ready"], 1)
                        if t == HT - 1:
                            pe.nop().then_inc(S["cb_done"], 1)
                    elif t == HT - 1:
                        ins.then_inc(S["cb_done"], 1)
                if cb + 2 < NT:
                    a_transposes(("a", cb + 2, 0))
                a_transposes(("a", cb, 1))

            def n_transposes(t):
                b = t_begin(("n", t))
                pe.wait_ge(S["xn2_done"], t + 1)
                v = xn2[:, t % HT, :].rearrange("r (p k) -> r k p", k=K)
                for k in range(K):
                    ins = pe.transpose(b[:, k * P:(k + 1) * P], v[:, k], ident[:, :])
                ins.then_inc(S["tr_ready"], 1)

            def logits_transposed(h):
                b = t_begin(("lgT", h))
                if h == 0:
                    pe.wait_ge(S["split_hi"], 2 * K)
                pe.wait_ge(S["tr_done"], LO.index(("n", h * HT + HT - 1)) + 1)
                split_product(b[0:5 * G, :], [(wrgh[:, k, :], wrgl[:, k, :], xTh[:, h, k, :], xTl[:, h, k, :])
                                              for k in range(K)]).then_inc(S["tr_ready"], 1)

            def logits(h):
                b = t_begin(("logits", h))
                pe.wait_ge(S["lgT_done"], h + 1)
                for s in range(HT):
                    ins = pe.transpose(b[:, s * 32:s * 32 + 5 * G], lgT[:, s * P:(s + 1) * P], ident[0:5 * G, 0:5 * G])
                ins.then_inc(S["tr_ready"], 1)

            def hidden_product(name, h, j):
                wh, wl = (w1h, w1l) if name == "h1" else (w3h, w3l)
                b = a_begin((name, h, j))
                c = slice(j * P, (j + 1) * P)
                split_product(b[:, :], [(wh[:, k, c], wl[:, k, c], xTh[:, h, k, :], xTl[:, h, k, :])
                                        for k in range(K)]).then_inc(S["acc_ready"], 1)

            def tw_transposes(h):
                b = t_begin(("tw", h))
                pe.wait_ge(S["tw_done"], HT * (h + 1))
                for s in range(HT):
                    ins = pe.transpose(b[0:E, s * P:(s + 1) * P], tw[:, s, :], ident[:, :])
                ins.then_inc(S["tr_ready"], 1)

            def tw_rows(h, j):
                b = a_begin(("tw", h, j))
                if j == 0:
                    pe.wait_ge(S["tr_done"], LO.index(("tw", h)) + 1)
                pe.matmul(b[:, :], expand[:, j, :], twTh[:, :], start=True, stop=False)
                pe.matmul(b[:, :], expand[:, j, :], twTl[:, :], start=False, stop=True).then_inc(S["acc_ready"], 1)

            def output(h):
                if h == 0:
                    pe.wait_ge(S["split_lo"], 3 * K)
                for t0 in (h * HT, h * HT + 2):
                    banks = [a_begin(("y", t)) for t in (t0, t0 + 1)]
                    for js in (range(K - 1), (K - 1,)):
                        if t0 == h * HT:
                            pe.wait_ge(S["g_lo"], h * K + js[-1] + 1)
                        for i in range(2):
                            r = slice((t0 + i) % HT * P, ((t0 + i) % HT + 1) * P)
                            for j in js:
                                for m, (a, w) in enumerate(((gTh, w2h), (gTl, w2h), (gTh, w2l))):
                                    ins = pe.matmul(banks[i][:, :], a[:, j, r], w[:, j, :],
                                                    start=j == 0 and m == 0, stop=j == K - 1 and m == 2)
                            if js[-1] == K - 1:
                                ins.then_inc(S["acc_ready"], 1)

            for t in range(HT, NT):
                a_begin(("gnn", t))
                for cb in range(NT):
                    if t == HT:
                        pe.wait_ge(S["tr_done"], LO.index(("a", cb, 1)) + 1)
                    ins = gnn_step(t, cb, cb == 0, cb == NT - 1)
                ins.then_inc(S["acc_ready"], 1)
                if t == HT + 1:
                    n_transposes(0)
                if t == HT + 2:
                    n_transposes(1)
                    n_transposes(2)
            n_transposes(3)
            pe.wait_ge(S["split_lo"], 2 * K)
            pe.wait_ge(S["c_expand"], 1)
            for h in range(2):
                logits_transposed(h)
                hidden_product("h1", h, 0)
                logits(h)
                hidden_product("h3", h, 0)
                if h:
                    output(0)
                hidden_product("h1", h, 1)
                hidden_product("h3", h, 1)
                if h == 0:
                    hidden_product("h1", h, 2)
                    hidden_product("h3", h, 2)
                tw_transposes(h)
                if h == 0:
                    n_transposes(4)
                tw_rows(h, 0)
                tw_rows(h, 1)
                if h:
                    hidden_product("h1", h, 2)
                    hidden_product("h3", h, 2)
                tw_rows(h, 2)
                hidden_product("h1", h, 3)
                if h == 0:
                    n_transposes(5)
                    n_transposes(6)
                hidden_product("h3", h, 3)
                if h == 0:
                    n_transposes(7)
                tw_rows(h, 3)
            output(1)

        @block.vector
        def _(v):
            step = [0]

            def link(ins):
                step[0] += 1
                ins.then_inc(S["chain"], 1)
                v.wait_ge(S["chain"], step[0])

            v.wait_ge(S["d_edges"], 48)
            v.tensor_scalar(lo_i[:, :], src_i[:, :], P - 1, None, ALU.bitwise_and).then_inc(S["prep"], 1)
            v.tensor_scalar(hi_i[:, :], src_i[:, :], 7, None, ALU.logical_shift_right).then_inc(S["prep"], 1)
            v.wait_ge(S["prep"], 2)
            v.tensor_copy(lo_f[:, :], lo_i[:, :]).then_inc(S["prep"], 1)
            v.scalar_tensor_tensor(comb[:, :], dst_i[:, :], float(SH), hi_i[:, :], ALU.mult, ALU.add).then_inc(S["prep"], 1)
            v.wait_ge(S["d_dstg"], 16)
            v.tensor_reduce(gmm[:, 0:1], dst_g[:, :], AX_X, ALU.min)
            link(v.tensor_reduce(gmm[:, 1:2], dst_g[:, :], AX_X, ALU.max))
            v.wait_ge(S["c_ident"], 1)
            for s in range(2):
                v.tensor_scalar(gdiag[:, s, :], ident[0:NG, 0:NG], gmm[:, s:s + 1], None, ALU.mult).then_inc(S["gdiag_done"], 1)
            def row_stats(t):
                v.bn_stats(stats[:, t, :], x_sb[:, t, :]).then_inc(S["chain"], 1)
                step[0] += 1
                v.wait_ge(S["chain"], step[0])
                return v.bn_aggr(mv[:, t, :], stats[:, t, :])

            def roots(i):
                v.wait_ge(S["std_done"], i + 1)
                r = slice(*ROOTS[i])
                link(v.reciprocal(rstd[:, r], std[:, r]))

            def tr_rest(use, dst_lo, src_psum, hi):
                v.wait_ge(S["tr_hi"], HI.index(use) + 1)
                return v.tensor_tensor(dst_lo, src_psum, hi.bitcast(F32), ALU.subtract).then_inc(S["tr_done"], 1)

            def statistics(i):
                for t in range(*ROOTS[i]):
                    v.wait_ge(d_x[t], 16)
                    ins = row_stats(t)
                ins.then_inc(S["std_req"], 1)

            def edges():
                eb, bb = tbank("edges"), tbank("base")
                v.wait_ge(S["tr_ready"], 1)
                v.tensor_copy(src_lo[:, :], eb[:, 0:P])
                link(v.tensor_copy(w_res[:, 0, :], eb[:, 2 * P:3 * P]))
                link(v.tensor_copy(w_parts[:, 0, :], w_res[:, 0, :]))
                link(v.tensor_tensor(w_res[:, 1, :], w_res[:, 0, :], w_parts[:, 0, :], ALU.subtract))
                link(v.tensor_copy(w_parts[:, 1, :], w_res[:, 1, :]))
                link(v.tensor_tensor(w_res[:, 2, :], w_res[:, 1, :], w_parts[:, 1, :], ALU.subtract))
                v.wait_ge(S["tr_ready"], 2)
                v.tensor_copy(gmax_row[:, :], bb[0:1, NG:2 * NG])
                link(v.tensor_scalar(base8[:, :], bb[:, 0:NG], float(SH), None, ALU.mult))
                v.tensor_tensor(combrel[:, :].rearrange("p (g i) -> p g i", i=GRP),
                                eb[:, P:2 * P].rearrange("p (g i) -> p g i", i=GRP),
                                base8[:, :].unsqueeze(2).broadcast_to([P, NG, GRP]), ALU.subtract).then_inc(S["tr_done"], 1)
                v.tensor_copy(offs[:, :], base8[0:1, :])
                link(v.tensor_tensor(span[:, :], gmax_row[:, :], bb[0:1, 0:NG], ALU.subtract))
                v.engine_nop().then_inc(S["tr_done"], 1)
                link(v.tensor_reduce(spanm[:, :], span[:, :], AX_X, ALU.max))
                v.wait_ge(S["c_kwin"], 1)
                link(v.tensor_scalar(kcmp[:, :], kwin[:, :], spanm[:, 0:1], None, ALU.is_le))
                link(v.tensor_reduce(nwin[:, :], kcmp[:, :], AX_X, ALU.add))
                link(v.tensor_scalar(nbody[:, :], nwin[:, :], 1.0, None, ALU.mult))
                v.engine_nop().then_inc(S["nbody_done"], 1)

            def normalize(t):
                if t >= 2:
                    v.wait_ge(S["tr_ready"], T.index(("x", t - 2)) + 1)
                v.tensor_scalar(xn1[:, t % 2, :], x_sb[:, t, :], mv[:, t, 0:1], rstd[:, t:t + 1],
                                ALU.subtract, ALU.mult).then_inc(S["xn_done"], 1)

            def onehots(b):
                v.tensor_tensor(onehot[:, b], iota_lo[:, :, :],
                                src_lo[:, b * BT:(b + 1) * BT].unsqueeze(1).broadcast_to([P, P, BT]),
                                ALU.is_equal).then_inc(S["onehot_done"], 1)

            def parts(b, slot):
                v.tensor_tensor(statn[:, slot, 0, :, :], onehot[:, b],
                                w_parts[:, 0, b * BT:(b + 1) * BT].unsqueeze(1).broadcast_to([P, P, BT]),
                                ALU.mult).then_inc(S["stat_done"], 1)

            def sweep(n, first):
                columns = [None] * NG

                def add(g):
                    v.wait_ge(S["grp_done"], n * NG + (g + 1))
                    if first and g == 0:
                        v.wait_ge(S["c_adj"], 1)
                    if g:
                        v.wait_ge(S["add_done"], n * NG + g)
                    a = adj[:, bass.ds(columns[g], WC)]
                    v.tensor_tensor(a, a, bank[2 + g % HB][:, 0:WC], ALU.add).then_inc(S["add_done"], 1)

                def windows(q):
                    og = offs[0:1, BG * q:BG * (q + 1)]
                    columns[BG * q:BG * (q + 1)] = nc.values_load_multi_w_load_instructions(
                        og, engines=[mybir.EngineType.DVE], min_val=0, max_val=NC)[1]
                    v.tensor_scalar(og, og, float(WC), float(NC), ALU.add, ALU.min)

                def stationaries(q):
                    if first:
                        if q == 0:
                            onehots(0)
                        if q + 1 < NB:
                            onehots(q + 1)
                        v.wait_ge(S["onehot_done"], q + 1)
                    parts(q, q % 3)
                    windows(q)

                if not first:
                    v.wait_ge(S["rel_done"], n)
                stationaries(0)
                stationaries(1)
                for q in range(NB):
                    for k in range(BG):
                        g = q * BG + k
                        for t in range(GRP * g, GRP * g + GRP):
                            ins = v.tensor_scalar(moving[:, t % BT, :], iota_win[:, :],
                                                  combrel[:, t:t + 1], None, ALU.is_equal)
                        ins.then_inc(S["mov_ready"], 1)
                        if g >= LAG:
                            add(g - LAG)
                        if k == LAG - 1 and q + 2 < NB:
                            stationaries(q + 2)
                        if first and (q, k) == (0, 0):
                            statistics(1)
                        if first and (q, k) == (0, BG - 1):
                            roots(1)
                        if first and k == BG - 1 and q in (1, 2):
                            for t in (2 * q + 2, 2 * q + 3):
                                v.wait_ge(d_x[t], 16)
                                ins = row_stats(t)
                            if q == 2:
                                ins.then_inc(S["std_req"], 1)
                        if first and (q, k) == (3, BG - 1):
                            roots(2)
                        if first and q % 2 == 0 and k == BG - 1 and q // 2 + 2 < NT:
                            normalize(q // 2 + 2)
                for g in range(NG - LAG, NG):
                    add(g)
                v.tensor_scalar(combrel[:, :], combrel[:, :], float(-WC), None, ALU.add)\
                    .then_inc(S["rel_done"], 1)
                v.wait_ge(S["add_done"], n * NG + NG)

            statistics(0)
            edges()
            roots(0)
            normalize(0)
            normalize(1)
            v.wait_ge(S["c_iota"], 2)
            sweep(0, True)
            sweeps = v.value_load(nbody[0:1, 0:1], min_val=1, max_val=N // WIN + 1)
            with v.If(sweeps > 1):
                with v.Fori(1, sweeps) as n:
                    sweep(n, False)
            v.engine_nop().then_inc(S["nbody_done"], 1)

            for u in T:
                if u[0] == "a":
                    if u[2] == 1:
                        v.wait_ge(S["cb_done"], u[1] + 1)
                    tr_rest(u, aTl[:, u[1], :], tbank(u)[:, :], aTh[:, u[1], :])

            v.wait_ge(S["d_small"], 16 * 5)

            def gnn_out(t):
                v.wait_ge(S["acc_ready"], A.index(("gnn", t)) + 1)
                ins = v.tensor_tensor(relu_in[:, t % 2, :], abank(("gnn", t))[:, :], biasb[:, :], ALU.add)
                ins.then_inc(S["acc_free"], 1)
                v.wait_ge(S["acc_free"], t + 1)
                link(v.scalar_tensor_tensor(x_sb[:, t, :], relu_in[:, t % 2, :], 0.0, x_sb[:, t, :], ALU.max, ALU.add))
                ins = row_stats(t)
                if t % HT == HT - 1:
                    ins.then_inc(S["std_req"], 1)

            def normalize2(t):
                if t >= HT:
                    v.wait_ge(S["tr_ready"], T.index(("n", t - HT)) + 1)
                v.tensor_scalar(xn2[:, t % HT, :], x_sb[:, t, :], mv[:, t, 0:1], rstd[:, t:t + 1],
                                ALU.subtract, ALU.mult).then_inc(S["xn2_done"], 1)

            def n_rest(t):
                r = slice(t % HT * P, (t % HT + 1) * P)
                tr_rest(("n", t), xTl[:, t // HT, :, r], tbank(("n", t))[:, :].rearrange("p (k r) -> p k r", k=K),
                        xTh[:, t // HT, :, r])

            def routing(h):
                v.wait_ge(S["tr_ready"], T.index(("logits", h)) + 1)
                lb = tbank(("logits", h))[:, 0:HT * 32].rearrange("p (s a) -> p s a", s=HT)[:, :, 0:5 * G]
                v.tensor_tensor(lg[:, :, :].rearrange("p (s a) e -> p s (a e)", s=HT), lb,
                                brg[:, :].unsqueeze(1).broadcast_to([P, HT, 5 * G]), ALU.add).then_inc(S["tr_done"], 1)
                v.wait_ge(S["tr_done"], LO.index(("logits", h)) + 1)

                def over(a):
                    return a[:, :].unsqueeze(2).broadcast_to([P, NGR, G])

                link(v.tensor_reduce(gm[:, :], lg[:, :, :], AX_X, ALU.max))
                v.tensor_tensor(gc[:, :, :], lg[:, :, :], over(gm), ALU.subtract).then_inc(S["exp_req"], 1)
                v.wait_ge(S["exp_done"], h + 1)
                link(v.tensor_reduce(gs[:, :], ge[:, :, :], AX_X, ALU.add))
                link(v.reciprocal(gr[:, :], gs[:, :]))
                link(v.tensor_tensor(gp[:, :, :], ge[:, :, :], over(gr), ALU.mult))
                pj = gp[:, :, :].unsqueeze(2).broadcast_to([P, NGR, G, G])
                pi = gp[:, :, :].unsqueeze(3).broadcast_to([P, NGR, G, G])
                v.tensor_tensor(gt[:, :, :, :], pj, pi, ALU.is_gt)
                link(v.tensor_tensor(eq[:, :, :, :], pj, pi, ALU.is_equal))
                link(v.tensor_tensor(eq[:, :, :, :].rearrange("p a i j -> p a (i j)"),
                                     eq[:, :, :, :].rearrange("p a i j -> p a (i j)"),
                                     tie[:, :, :].rearrange("p i j -> p (i j)").unsqueeze(1).broadcast_to([P, NGR, G * G]),
                                     ALU.mult))
                link(v.tensor_tensor(gt[:, :, :, :], gt[:, :, :, :], eq[:, :, :, :], ALU.add))
                link(v.tensor_reduce(rank[:, :, :], gt[:, :, :, :], AX_X, ALU.add))
                link(v.scalar_tensor_tensor(p2[:, :, :], rank[:, :, :], 1.0, gp[:, :, :], ALU.is_le, ALU.mult))
                link(v.tensor_reduce(gs[:, :], p2[:, :, :], AX_X, ALU.add))
                link(v.tensor_scalar(gr[:, :], gs[:, :], 0.9, None, ALU.is_le))
                link(v.tensor_tensor(m2[:, :, :], rank[:, :, :], over(gr), ALU.is_le))
                link(v.tensor_tensor(p2[:, :, :], gp[:, :, :], m2[:, :, :], ALU.mult))
                link(v.tensor_reduce(gs[:, :], p2[:, :, :], AX_X, ALU.add))
                link(v.tensor_scalar(gs[:, :], gs[:, :], 1e-9, None, ALU.add))
                link(v.reciprocal(gr[:, :], gs[:, :]))
                link(v.tensor_tensor(p2[:, :, :], p2[:, :, :], over(gr), ALU.mult))
                w5 = p2[:, :, :].rearrange("p (s a) e -> p s a e", s=HT)
                for s in range(HT):
                    wg = w5[:, s, 0, :].unsqueeze(2).broadcast_to([P, G, G])
                    v.scalar_tensor_tensor(tw[:, s, :].rearrange("p (g e) -> p g e", g=G), w5[:, s, 1:5, :],
                                                 0.5, wg, ALU.mult, ALU.mult).then_inc(S["tw_done"], 1)

            def hide(h, j):
                v.wait_ge(S["silu_done"], K * h + j + 1)
                v.wait_ge(S["acc_ready"], A.index(("h3", h, j)) + 1)
                v.tensor_tensor(hidden[:, j, :], silu[:, j, :], abank(("h3", h, j))[:, :],
                                ALU.mult).then_inc(S["acc_free"], 2)

            def gate(h, j):
                u = A.index(("tw", h, j))
                v.wait_ge(S["acc_ready"], u + 1)
                v.wait_ge(S["acc_free"], A.index(("h3", h, j)) + 1)
                v.tensor_tensor(gated[:, j, :], hidden[:, j, :], abank(("tw", h, j))[:, :],
                                ALU.mult).then_inc(S["acc_free"], 1)
                v.wait_ge(S["acc_free"], u + 1)
                v.engine_nop().then_inc(S["gated_done"], 1)

            def gate_rest(h, j):
                v.wait_ge(S["g_hi"], K * h + j + 1)
                v.tensor_tensor(gTl[:, j, :], gated[:, j, :], gTh[:, j, :].bitcast(F32),
                                ALU.subtract).then_inc(S["g_lo"], 1)

            def finish(t):
                u = A.index(("y", t))
                v.wait_ge(S["acc_ready"], u + 1)
                if t >= 4:
                    v.wait_ge(d_out[t % 4], 16 * (t // 4))
                v.tensor_tensor(y_sb[:, t % 4, :], abank(("y", t))[:, :], x_sb[:, t, :], ALU.add).then_inc(S["acc_free"], 1)
                v.wait_ge(S["acc_free"], u + 1)
                v.engine_nop().then_inc(S["y_done"], 1)

            for t in range(HT):
                gnn_out(t)
            roots(3)
            v.wait_ge(S["split_lo"], 2 * K)
            for t in range(HT):
                normalize2(t)
            n_rest(0)
            n_rest(1)
            gnn_out(HT)
            n_rest(2)
            gnn_out(HT + 1)
            n_rest(3)
            gnn_out(HT + 2)
            routing(0)
            gnn_out(HT + 3)
            roots(4)
            for h in range(2):
                hide(h, 0)
                if h:
                    for t in range(HT):
                        finish(t)
                hide(h, 1)
                if h == 0:
                    hide(h, 2)
                    for t in range(HT, NT):
                        normalize2(t)
                v.wait_ge(S["tr_hi"], HI.index(("tw", h)) + 1)
                v.tensor_tensor(twTl[:, :], tbank(("tw", h))[0:E, :], twTh[:, :].bitcast(F32),
                                ALU.subtract).then_inc(S["tr_done"], 1)
                gate(h, 0)
                gate_rest(h, 0)
                if h == 0:
                    n_rest(4)
                gate(h, 1)
                gate_rest(h, 1)
                if h == 0:
                    n_rest(5)
                else:
                    hide(h, 2)
                gate(h, 2)
                gate_rest(h, 2)
                if h == 0:
                    n_rest(6)
                    n_rest(7)
                hide(h, 3)
                gate(h, 3)
                gate_rest(h, 3)
                if h == 0:
                    routing(1)
            for t in range(HT, NT):
                finish(t)


_INS = ["x", "src", "dst", "edge_weight", "L0_gnn_W", "L0_gnn_bias", "L0_ffn_Wr", "L0_ffn_br", "L0_ffn_Wgate",
        "L0_ffn_bgate", "L0_ffn_W1", "L0_ffn_W3", "L0_ffn_W2"]


def kernel(**inputs):
    import numpy as _np
    import concourse.bacc as _bacc
    from concourse import mybir as _mybir
    from concourse.bass_utils import run_bass_kernel_spmd as _run

    nc = _bacc.Bacc("TRN2", target_bir_lowering=False, num_devices=1)
    arrays, args = {}, []
    for name in _INS:
        a = _np.ascontiguousarray(inputs[name])
        arrays[f"in_{name}_dram"] = a
        args.append(nc.dram_tensor(f"in_{name}_dram", a.shape, _mybir.dt.from_np(a.dtype), kind="ExternalInput").ap())
    args.append(nc.dram_tensor("out_0_dram", (N, D), F32, kind="ExternalOutput").ap())
    gnn_ffn(nc, *args)
    r = _run(nc, [arrays], core_ids=[0])
    return r.results[0]["out_0_dram"]
```

```python
from contextlib import ExitStack

import concourse.bass as bass
from concourse import mybir

ALU = mybir.AluOpType
ACT = mybir.ActivationFunctionType
AX_X = mybir.AxisListType.X
F32 = mybir.dt.float32
F32R = mybir.dt.float32r
BF16 = mybir.dt.bfloat16
I32 = mybir.dt.int32

P = 128
N = 1024
D = 512
NE = 16384
E = 16
G = 4
NT = N // P
HT = NT // 2
K = D // P
ET = NE // P
GRP = 2
NG = ET // GRP
SH = N // P
WIN = 36
WC = WIN * SH
BT = 8
IL = 4
BG = BT // GRP
NC = N * SH
NB = ET // BT
ADJ_V = NC // 4
E2 = 32 + E
ROOTS = [(0, 2), (2, 4), (4, 8), (0, 4), (4, 8)]
LAG = 2
HB = 4
AR = 6
EPS = 1e-5


def gnn_ffn(nc, x, src, dst, edge_weight, w_gnn, bias_gnn, w_r, b_r, w_gate, b_gate, w1, w3, w2, out):
    with ExitStack() as ctx:
        def sb(name, shape, dt):
            return ctx.enter_context(nc.sbuf_tensor(name, shape, dt))

        def sem(name):
            return ctx.enter_context(nc.semaphore(name))

        def region(name, size):
            slab = sb(name, [P, size // 4], F32)
            return nc.sbuf_base - size if nc.sbuf_base - size >= 0 else slab

        def at(name, shape, dt, offset):
            return nc.alloc_sbuf_tensor_at(name, shape, dt, offset=offset)

        KB = 1024
        adj_at = region("adj_region", 34048)
        adj = at("adj", [P, NC + WC], F32, adj_at)
        xTh = at("xTh", [P, 2, K, HT * P], F32R, adj_at)
        xTl = at("xTl", [P, 2, K, HT * P], F32R, adj_at + 16 * KB)
        aT_at = region("aT_region", 32 * KB)
        aTh = at("aTh", [P, NT, HT * P], F32R, aT_at)
        aTl = at("aTl", [P, NT, HT * P], F32R, aT_at + 16 * KB)
        wgh = at("wgh", [P, K, D], F32R, aT_at)
        wgl = at("wgl", [P, K, D], F32R, aT_at + 8 * KB)
        nTh = at("nTh", [P, 2, K, P], F32R, aT_at + 16 * KB)
        nTl = at("nTl", [P, 2, K, P], F32R, aT_at + 20 * KB)
        expf = at("expf", [E2, 4, P], F32, aT_at + 24 * KB)
        src_i, dst_i, lo_i, hi_i, ew, lo_f, comb = (
            at(n, [P, P], dt, aT_at + 26 * KB + 512 * i) for i, (n, dt) in enumerate(
                [("src_i", I32), ("dst_i", I32), ("lo_i", I32), ("hi_i", I32), ("ew", F32), ("lo_f", F32), ("comb", F32)]))
        raw = at("raw", [P, 2, D], F32, aT_at + 26 * KB)
        silu = at("silu", [P, K, HT * P], F32, aT_at)
        hidden = at("hidden", [P, K, HT * P], F32, aT_at + 8 * KB)
        gated = at("gated", [P, K, HT * P], F32, aT_at + 16 * KB)
        dst_g = at("dst_g", [NG, GRP * P], I32, aT_at + 30 * KB)
        gdiag = at("gdiag", [NG, 2, NG], F32, aT_at + 31 * KB)
        hist_at = region("hist_region", 24 * KB)
        statn = at("statn", [P, 3, 3, BT // IL, P, IL], BF16, hist_at)
        moving = at("moving", [P, BG, WC, GRP], BF16, hist_at + 18 * KB)
        gTh = at("gTh", [P, K, HT * P], F32R, hist_at)
        gTl = at("gTl", [P, K, HT * P], F32R, hist_at + 8 * KB)
        relu_in = at("relu_in", [P, 2, D], F32, hist_at + 16 * KB)
        twT = at("twT", [E2, HT * P], F32R, hist_at + 20 * KB)
        hw_at = region("hw_region", 32 * KB)
        hwh = at("hwh", [P, NT, D], F32R, hw_at)
        hwl = at("hwl", [P, NT, D], F32R, hw_at + 16 * KB)
        y_sb = at("y_sb", [P, 4, D], F32, hw_at)
        lgT = at("lgT", [10 * G, HT * P], F32, hw_at + 8 * KB)
        w2h = at("w2h", [P, K, D], F32R, hw_at + 16 * KB)
        w2l = at("w2l", [P, K, D], F32R, hw_at + 24 * KB)
        w13_at = region("w13_region", 32 * KB)
        w1h, w1l, w3h, w3l = (at(n, [P, K, D], F32R, w13_at + 8 * KB * i)
                              for i, n in enumerate(("w1h", "w1l", "w3h", "w3l")))
        onehot = at("onehot", [P, NB, BT // IL, P, IL], BF16, w13_at)
        st_at = region("stage_region", 16 * KB)
        stage = [at(f"stage{i}", [P, K * D], F32, st_at + 8 * KB * i) for i in range(2)]
        xn1 = at("xn1", [P, 2, D], F32, st_at + 8 * KB)
        xn2 = at("xn2", [P, HT, D], F32, st_at)

        x_sb = sb("x_sb", [P, NT, D], F32)
        wrg_raw = sb("wrg_raw", [P, 5, K, G], F32)
        wrg2 = sb("wrg2", [P, K, 2, 5 * G], F32R)
        brg = sb("brg", [P, 5 * G], F32)
        biasb = sb("biasb", [P, D], F32)
        ident = sb("ident", [P, P], F32)
        ones = sb("ones", [NG, P], F32)
        epsb = sb("epsb", [P, 1], F32)
        iota_lo = sb("iota_lo", [P, P, IL], BF16)
        iota_win = sb("iota_win", [P, WC, GRP], BF16)
        tie = sb("tie", [P, G, G], F32)
        expand = sb("expand", [E2, 4, P], F32R)
        gmm = sb("gmm", [NG, 2], F32)
        base8 = sb("base8", [P, NG], F32)
        gmax_row = sb("gmax_row", [1, NG], F32)
        span = sb("span", [1, NG], F32)
        spanm = sb("spanm", [1, 1], F32)
        kwin = sb("kwin", [1, N // WIN + 1], F32)
        kcmp = sb("kcmp", [1, N // WIN + 1], F32)
        nwin = sb("nwin", [1, 1], F32)
        nbody = sb("nbody", [1, 1], I32)
        offs = sb("offs", [1, NG], I32)
        combrel = sb("combrel", [P, ET], F32)
        column = sb("column", [P, ET], BF16)
        src_lo = sb("src_lo", [P, ET], BF16)
        w_res = sb("w_res", [P, 3, ET], F32)
        w_parts = sb("w_parts", [P, 2, ET], BF16)
        stats = sb("stats", [P, NT, 6], F32)
        mv = sb("mv", [P, NT, 2], F32)
        std = sb("std", [P, NT], F32)
        rstd = sb("rstd", [P, NT], F32)
        bias_n = sb("bias_n", [P, NT], F32)
        NGR = HT * 5
        lg = sb("lg", [P, NGR, G], F32)
        gm = sb("gm", [P, NGR], F32)
        gc = sb("gc", [P, NGR, G], F32)
        ge = sb("ge", [P, NGR, G], F32)
        gs = sb("gs", [P, NGR], F32)
        gr = sb("gr", [P, NGR], F32)
        gp = sb("gp", [P, NGR, G], F32)
        gt = sb("gt", [P, NGR, G, G], F32)
        eq = sb("eq", [P, NGR, G, G], F32)
        rank = sb("rank", [P, NGR, G], F32)
        m2 = sb("m2", [P, NGR, G], F32)
        p2 = sb("p2", [P, NGR, G], F32)
        tw = sb("tw", [P, HT, E2], F32)

        bank = [ctx.enter_context(nc.psum_tensor(f"bank{i}", [P, 512], F32)) for i in range(8)]

        names = """d_dstg d_edges d_wg d_w1 d_w3 d_w2 d_small
                   c_ident0 c_ident c_ones c_iota c_adj c_tie0 c_tie c_exp0 c_exp1 c_exp c_expand c_kwin
                   prep gdiag_done tr_ready tr_hi tr_done raw_done raw_rest c_table wg_hi wg_lo std_req std_done xn_done
                   hw_ready split_hi split_lo nbody_done
                   parts_done onehot_done shifted centered norm_ready stat_done second_done rest_done mov_ready grp_done add_done
                   acc_ready acc_free cb_done chain lgT_done exp_req exp_done xn2_done
                   tw_done silu_done gated_done g_hi g_lo y_done"""
        S = {n: sem(n) for n in names.split()}
        d_x = [sem(f"d_x{t}") for t in range(NT)]
        d_out = [sem(f"d_out{i}") for i in range(4)]

        T = ["edges", "base"] + [("x", t) for t in range(NT)]
        T += [("a", 0, 0), ("a", 1, 0)]
        for cb in range(NT):
            if cb + 2 < NT:
                T.append(("a", cb + 2, 0))
            T.append(("a", cb, 1))
        T += [("n", t) for t in range(HT)] + [("lgT", 0), ("logits", 0)] + [("n", t) for t in range(HT, NT)]
        T += [("tw", 0), ("lgT", 1), ("logits", 1), ("tw", 1)]
        HI = [u for u in T if u[0] in ("a", "n", "tw")]
        LO = [u for u in T if u[0] not in ("x", "lgT")]
        R = [("x", 0), ("x", 1)]
        for t in range(2, NT):
            R += [("hw", t - 2), ("x", t)]
        R += [("hw", NT - 2), ("hw", NT - 1)]

        def after_batch(q):
            if q == 1:
                return ("x", 0)
            return ("x", q // 2) if q % 2 == 0 else ("hw", (q - 3) // 2)

        A = [("gnn", t) for t in range(NT)]
        A += [(n, 0, j) for j in range(K) for n in ("h1", "h3")] + [("tw", 0, j) for j in range(K)]
        A += [("h1", 1, 0), ("h3", 1, 0)] + [("y", t) for t in range(HT)] + [("h1", 1, 1), ("h3", 1, 1)]
        A += [("tw", 1, 0), ("tw", 1, 1), ("h1", 1, 2), ("h3", 1, 2), ("tw", 1, 2), ("h1", 1, 3), ("tw", 1, 3), ("h3", 1, 3)]
        A += [("y", t) for t in range(HT, NT)]

        def factors(h, j):
            return (("tw", h, j), ("h3", h, j)) if (h, j) == (1, 3) else (("h3", h, j), ("tw", h, j))

        def over_columns(a):
            return a.rearrange("p (b i) -> p b i", i=IL).unsqueeze(2).broadcast_to([P, BT // IL, P, IL])

        def tbank(u):
            return bank[T.index(u) % 2]

        def abank(u):
            return bank[2 + A.index(u) % AR]

        block = ctx.enter_context(nc.Block())

        @block.sync
        def _(sp):
            sp.dma_start(dst_g[:, :], dst.rearrange("(g e) -> g e", g=NG)).then_inc(S["d_dstg"], 16)
            sp.dma_start(src_i[:, :], src.rearrange("(t e) -> t e", t=ET)).then_inc(S["d_edges"], 16)
            for t in range(NT):
                sp.dma_start(x_sb[:, t, :], x[t * P:(t + 1) * P, :]).then_inc(d_x[t], 16)
                if t == 1:
                    sp.dma_start(stage[0][:, :].rearrange("p (k n) -> p k n", k=K),
                                 w_gnn.rearrange("(k p) n -> p k n", k=K)).then_inc(S["d_wg"], 16)
            small = S["d_small"]
            sp.dma_start(wrg_raw[:, 0, :, :], w_r.rearrange("(p k) e -> p k e", k=K)).then_inc(small, 16)
            sp.dma_start(wrg_raw[:, 1:1 + G, :, :].rearrange("p g k e -> p g (k e)"),
                         w_gate.rearrange("g (p k) e -> p g (k e)", k=K)).then_inc(small, 16)
            sp.dma_start(brg[:, 0:G], b_r.rearrange("(a e) -> a e", a=1).broadcast_to([P, G])).then_inc(small, 16)
            sp.dma_start(brg[:, G:5 * G], b_gate.rearrange("(a g) e -> a (g e)", a=1).broadcast_to([P, G * G]))\
              .then_inc(small, 16)
            sp.dma_start(biasb[:, :], bias_gnn.rearrange("(a n) -> a n", a=1).broadcast_to([P, D])).then_inc(small, 16)
            sp.wait_ge(S["wg_lo"], K)
            sp.dma_start(stage[0][:, :].rearrange("p (e a) -> p e a", e=E),
                         w3.rearrange("e (p k) h -> p e (k h)", k=K)).then_inc(S["d_w3"], 16)
            sp.wait_ge(S["tr_ready"], T.index(("x", NT - 1)) + 1)
            sp.dma_start(stage[1][:, :].rearrange("p (e a) -> p e a", e=E),
                         w1.rearrange("e (p k) h -> p e (k h)", k=K)).then_inc(S["d_w1"], 16)
            sp.wait_ge(S["split_lo"], K)
            sp.dma_start(stage[1][:, :].rearrange("p (j n) -> p j n", j=K),
                         w2.rearrange("e h n -> (e h) n").rearrange("(j p) n -> p j n", p=P)).then_inc(S["d_w2"], 16)
            for t in range(NT):
                sp.wait_ge(S["y_done"], t + 1)
                sp.dma_start(out[t * P:(t + 1) * P, :], y_sb[:, t % 4, :]).then_inc(d_out[t % 4], 16)
            for i in range(4):
                sp.wait_ge(d_out[i], 16 * (NT // 4))

        @block.gpsimd
        def _(g):
            g.memset(ident[:, :], 0.0).then_inc(S["c_ident0"], 1)
            g.memset(ones[:, :], 1.0).then_inc(S["c_ones"], 1)
            g.memset(epsb[:, :], EPS).then_inc(S["c_ones"], 1)
            g.wait_ge(S["c_ident0"], 1)
            g.affine_select(out=ident[:, :], in_=ident[:, :], compare_op=ALU.not_equal, fill=1.0, base=0,
                            pattern=[[-1, P]], channel_multiplier=1).then_inc(S["c_ident"], 1)
            g.iota(kwin[:, :], pattern=[[WIN, N // WIN + 1]], base=0, channel_multiplier=0,
                   allow_small_or_imprecise_dtypes=True).then_inc(S["c_kwin"], 1)
            g.iota(iota_lo[:, :, :], pattern=[[1, P], [0, IL]], base=0, channel_multiplier=0,
                   allow_small_or_imprecise_dtypes=True).then_inc(S["c_iota"], 1)
            g.iota(iota_win[:, :, :], pattern=[[1, WC], [0, GRP]], base=-WC // 2, channel_multiplier=0,
                   allow_small_or_imprecise_dtypes=True).then_inc(S["c_iota"], 1)
            g.memset(adj[:, ADJ_V:], 0.0).then_inc(S["c_adj"], 1)

            def gnn_weight_rest(k):
                g.wait_ge(S["wg_hi"], k + 1)
                g.tensor_tensor(wgl[:, k, :], stage[0][:, k * D:(k + 1) * D], wgh[:, k, :].bitcast(F32),
                                ALU.subtract).then_inc(S["wg_lo"], 1)

            def routing_constants(i):
                if i == 0:
                    g.memset(tie[:, :, :], 1.0).then_inc(S["c_tie0"], 1)
                    g.wait_ge(S["c_tie0"], 1)
                    g.affine_select(out=tie[:, :, :], in_=tie[:, :, :], compare_op=ALU.is_gt, fill=0.0, base=0,
                                    pattern=[[1, G], [-1, G]], channel_multiplier=0).then_inc(S["c_tie"], 1)
                    g.memset(tw[:, :, :], 0.0).then_inc(S["c_tie"], 1)
                if i == 1:
                    g.memset(expf[:, :, :], 1.0).then_inc(S["c_exp0"], 1)
                    g.wait_ge(S["c_exp0"], 1)
                    g.affine_select(out=expf[:, :, :], in_=expf[:, :, :], compare_op=ALU.is_ge, fill=0.0, base=0,
                                    pattern=[[P, 4], [1, P]], channel_multiplier=-32).then_inc(S["c_exp1"], 1)
                    g.wait_ge(S["c_exp1"], 1)
                if i == 2:
                    g.affine_select(out=expf[:, :, :], in_=expf[:, :, :], compare_op=ALU.is_ge, fill=0.0, base=31,
                                    pattern=[[-P, 4], [-1, P]], channel_multiplier=32).then_inc(S["c_exp"], 1)
                    g.wait_ge(S["c_exp"], 1)
                if i == 3:
                    g.tensor_copy(expand[:, :, :], expf[:, :, :]).then_inc(S["c_expand"], 1)

            def load_sweeps():
                g.wait_ge(S["nbody_done"], 1)
                return g.value_load(nbody[0:1, 0:1], min_val=1, max_val=N // WIN + 1)

            def rest_of(use):
                what, t = use
                m = R.index(use)
                g.wait_ge(S["raw_done"], m + 1)
                if what == "x":
                    hi, lo = nTh[:, t % 2, :, :].rearrange("p k r -> p (k r)"), nTl[:, t % 2, :, :].rearrange("p k r -> p (k r)")
                else:
                    hi, lo = hwh[:, t, :], hwl[:, t, :]
                g.tensor_tensor(lo, raw[:, m % 2, :], hi.bitcast(F32), ALU.subtract).then_inc(S["raw_rest"], 1)

            def sweep(n, first):
                for q in range(NB):
                    if first and q == 0:
                        g.wait_ge(S["parts_done"], 1)
                        g.wait_ge(S["onehot_done"], 1)
                    else:
                        g.wait_ge(S["stat_done"], n * NB + (q + 1))
                    g.tensor_tensor(statn[:, q % 3, 1], onehot[:, q], over_columns(w_parts[:, 1, q * BT:(q + 1) * BT]),
                                    ALU.mult).then_inc(S["second_done"], 1)
                    if first and q == 0:
                        for k in range(1, K):
                            gnn_weight_rest(k)
                    if first and q:
                        rest_of(after_batch(q))
                    if first and q in (6, 8, 10, 12):
                        routing_constants(q // 2 - 3)
                if first:
                    rest_of(("hw", NT - 1))

            gnn_weight_rest(0)
            sweep(0, True)
            sweeps = load_sweeps()
            with g.If(sweeps > 1):
                with g.Fori(1, sweeps) as n:
                    sweep(n, False)
            g.wait_ge(S["d_small"], 16 * 5)
            wrg = wrg_raw[:, :, :, :].rearrange("p s k e -> p k s e")
            n = 0
            for k in range(K):
                hi = wrg2[:, k, 0, :].rearrange("p (s e) -> p s e", s=5)
                lo = wrg2[:, k, 1, :].rearrange("p (s e) -> p s e", s=5)
                g.tensor_copy(hi, wrg[:, k]).then_inc(S["split_hi"], 1)
                n += 1
                g.wait_ge(S["split_hi"], n)
                g.tensor_tensor(lo, wrg[:, k], hi.bitcast(F32), ALU.subtract).then_inc(S["split_hi"], 1)
                n += 1
            for which, st, hi_t, lo_t in (("d_w1", 1, w1h, w1l), ("d_w3", 0, w3h, w3l), ("d_w2", 1, w2h, w2l)):
                g.wait_ge(S[which], 16)
                if which == "d_w1":
                    g.wait_ge(S["nbody_done"], 2)
                    g.wait_ge(S["tr_hi"], HI.index(("a", 0, 0)) + 1)
                if which == "d_w2":
                    g.wait_ge(S["acc_ready"], NT)
                for k in range(K):
                    if which == "d_w2":
                        whole, hi, lo = stage[st][:, k * D:(k + 1) * D], hi_t[:, k, :], lo_t[:, k, :]
                    else:
                        whole = stage[st][:, :].rearrange("p (e k h) -> p k e h", e=E, k=K)[:, k]
                        hi = hi_t[:, k, :].rearrange("p (e h) -> p e h", e=E)
                        lo = lo_t[:, k, :].rearrange("p (e h) -> p e h", e=E)
                    g.tensor_copy(hi, whole).then_inc(S["split_hi"], 1)
                    n += 1
                    g.wait_ge(S["split_hi"], n)
                    g.tensor_tensor(lo, whole, hi.bitcast(F32), ALU.subtract).then_inc(S["split_lo"], 1)

        @block.scalar
        def _(act):
            def round_hi(use, dst_hi, src_psum):
                act.wait_ge(S["tr_ready"], T.index(use) + 1)
                act.copy(dst_hi, src_psum).then_inc(S["tr_hi"], 1)

            def roots(i):
                act.wait_ge(S["std_req"], i + 1)
                r = slice(*ROOTS[i])
                act.activation(std[:, r], mv[:, r, 1], ACT.Sqrt, bias=epsb[:, 0:1]).then_inc(S["std_done"], 1)

            act.dma_start(dst_i[:, :], dst.rearrange("(t e) -> t e", t=ET)).then_inc(S["d_edges"], 16)
            act.dma_start(ew[:, :], edge_weight.rearrange("(t e) -> t e", t=ET)).then_inc(S["d_edges"], 16)
            act.wait_ge(S["c_ones"], 2)
            act.activation(std[:, 0:1], epsb[:, 0:1], ACT.Sqrt).then_inc(S["c_table"], 1)
            act.wait_ge(S["c_table"], 1)
            roots(0)
            act.wait_ge(S["d_wg"], 16)

            def gnn_weight_rounded(ks):
                for k in ks:
                    act.copy(wgh[:, k, :], stage[0][:, k * D:(k + 1) * D]).then_inc(S["wg_hi"], 1)

            gnn_weight_rounded((0, 1))

            def copy_and_round(use):
                what, t = use
                m = R.index(use)
                if what == "x":
                    act.wait_ge(S["tr_ready"], T.index(use) + 1)
                    if t >= 2:
                        act.wait_ge(S["hw_ready"], t - 1)
                    src_psum, hi = tbank(use)[:, :], nTh[:, t % 2, :, :].rearrange("p k r -> p (k r)")
                else:
                    act.wait_ge(S["hw_ready"], t + 1)
                    src_psum, hi = bank[6 + t % 2][:, :], hwh[:, t, :]
                act.copy(hi, src_psum)
                if m >= 2:
                    act.wait_ge(S["raw_rest"], m - 1)
                act.copy(raw[:, m % 2, :], src_psum).then_inc(S["raw_done"], 1)

            def normalize(t):
                act.wait_ge(S["norm_ready"], 1 if t < 4 else 2)
                act.wait_ge(S["tr_ready"], T.index(("x", t - 2)) + 1)
                act.activation(xn1[:, t % 2, :], x_sb[:, t, :], ACT.Identity, scale=rstd[:, t:t + 1],
                               bias=bias_n[:, t:t + 1]).then_inc(S["xn_done"], 1)

            def third_parts(b, slot):
                for i in range(BT):
                    ins = act.activation(statn[:, slot, 2, i // IL, :, i % IL], onehot[:, b, i // IL, :, i % IL], ACT.Copy,
                                         scale=w_res[:, 2, b * BT + i:b * BT + i + 1])
                ins.then_inc(S["rest_done"], 1)

            def sweep(n, first):
                for q in range(NB):
                    if first and q == 0:
                        act.wait_ge(S["parts_done"], 1)
                        act.wait_ge(S["onehot_done"], 1)
                    else:
                        act.wait_ge(S["stat_done"], n * NB + (q + 1))
                    third_parts(q, q % 3)
                    if first and q == 0:
                        gnn_weight_rounded((2, 3))
                    if first and q == 2:
                        roots(1)
                    if first and q == 6:
                        roots(2)
                    if first and q:
                        copy_and_round(after_batch(q))
                    if first and q % 2 == 1 and 2 <= (q + 1) // 2 < NT:
                        normalize((q + 1) // 2)
                    if first and q == NB - 1:
                        loaded.append(load_sweeps())
                        act.wait_ge(S["c_expand"], 1)
                        act.copy(expand[32:E2, :, :], expf[0:E, :, :]).then_inc(S["c_expand"], 1)
                if first:
                    copy_and_round(("hw", NT - 1))

            loaded = []

            def load_sweeps():
                act.wait_ge(S["nbody_done"], 1)
                return act.value_load(nbody[0:1, 0:1], min_val=1, max_val=N // WIN + 1)

            sweep(0, True)
            sweeps = loaded[0]
            with act.If(sweeps > 1):
                with act.Fori(1, sweeps) as n:
                    sweep(n, False)
            for u in T:
                if u[0] == "a":
                    if u[2] == 1:
                        act.wait_ge(S["cb_done"], u[1] + 1)
                    round_hi(u, aTh[:, u[1], :], tbank(u)[:, :])

            def n_round(t):
                round_hi(("n", t), xTh[:, t // HT, :, (t % HT) * P:(t % HT + 1) * P],
                         tbank(("n", t))[:, :].rearrange("p (k r) -> p k r", k=K))

            def gate(n):
                h, j = divmod(n, K)
                act.wait_ge(S["acc_ready"], A.index(("h1", h, j)) + 1)
                if h:
                    act.wait_ge(S["acc_free"], A.index(("h3", 0, j)) + 1)
                act.activation(silu[:, j, :], abank(("h1", h, j))[:, :], ACT.Silu).then_inc(S["silu_done"], 1)

            def g_round(n):
                act.wait_ge(S["gated_done"], n + 1)
                act.copy(gTh[:, n % K, :], gated[:, n % K, :]).then_inc(S["g_hi"], 1)

            roots(3)
            for t in range(HT):
                n_round(t)

            def copy_logits(h):
                act.wait_ge(S["tr_ready"], T.index(("lgT", h)) + 1)
                act.copy(lgT[:, :], tbank(("lgT", h))[0:10 * G, :]).then_inc(S["lgT_done"], 1)

            copy_logits(0)
            for h in range(2):
                if h == 0:
                    roots(4)
                act.wait_ge(S["exp_req"], h + 1)
                act.activation(ge[:, :, :], gc[:, :, :], ACT.Exp).then_inc(S["exp_done"], 1)
                if h == 0:
                    for j in range(3):
                        gate(j)
                    n_round(4)
                    n_round(5)
                    gate(3)
                    n_round(6)
                    n_round(7)
                    round_hi(("tw", 0), twT[:, :], tbank(("tw", 0))[0:E2, :])
                    copy_logits(1)
                    for j in range(K):
                        g_round(j)
                else:
                    gate(K)
                    gate(K + 1)
                    round_hi(("tw", 1), twT[:, :], tbank(("tw", 1))[0:E2, :])
                    g_round(K)
                    g_round(K + 1)
                    for n in (K + 2, K + 3):
                        gate(n)
                        g_round(n)

        @block.tensor
        def _(pe):
            used = [0, 0]

            def t_begin(use):
                assert T[used[0]] == use
                if used[0] >= 2:
                    before = T[used[0] - 2]
                    if before[0] == "x":
                        pe.wait_ge(S["raw_done"], R.index(before) + 1)
                    elif before[0] == "lgT":
                        pe.wait_ge(S["lgT_done"], before[1] + 1)
                    else:
                        pe.wait_ge(S["tr_done"], LO.index(before) + 1)
                used[0] += 1
                return tbank(use)

            def a_begin(use):
                assert A[used[1]] == use, (A[used[1]], use)
                if used[1] >= AR:
                    pe.wait_ge(S["acc_free"], used[1] - AR + 1)
                used[1] += 1
                return abank(use)

            def split_product(out_ap, pairs):
                n, last = 0, 3 * len(pairs) - 1
                for lh, ll, rh, rl in pairs:
                    for a, b in ((lh, rh), (ll, rh), (lh, rl)):
                        ins = pe.matmul(out_ap, a, b, start=n == 0, stop=n == last)
                        n += 1
                return ins

            pe.wait_ge(S["c_ident"], 1)
            pe.wait_ge(S["d_edges"], 48)
            pe.wait_ge(S["prep"], 4)
            b = t_begin("edges")
            pe.transpose(b[:, 0:P], lo_f[:, :], ident[:, :])
            pe.transpose(b[:, P:2 * P], comb[:, :], ident[:, :])
            pe.transpose(b[:, 2 * P:3 * P], ew[:, :], ident[:, :]).then_inc(S["tr_ready"], 1)
            b = t_begin("base")
            pe.wait_ge(S["c_ones"], 2)
            pe.wait_ge(S["gdiag_done"], 2)
            pe.matmul(b[:, 0:2 * NG], ones[:, :], gdiag[:, :, :].rearrange("p s g -> p (s g)"),
                      start=True, stop=True).then_inc(S["tr_ready"], 1)

            def x_transposes(t, k0):
                if k0 == 0:
                    t_begin(("x", t))
                    pe.wait_ge(S["xn_done"], t + 1)
                v = xn1[:, t % 2, :].rearrange("r (k p) -> r k p", k=K)
                for k in (k0, k0 + 1):
                    ins = pe.transpose(tbank(("x", t))[:, k * P:(k + 1) * P], v[:, k], ident[:, :])
                if k0 + 2 == K:
                    ins.then_inc(S["tr_ready"], 1)

            def x_product(t, sixth):
                if sixth == 0:
                    if t == 0:
                        pe.wait_ge(S["wg_lo"], K)
                    pe.wait_ge(S["raw_rest"], R.index(("x", t)) + 1)
                    if t >= 2:
                        pe.wait_ge(S["raw_done"], R.index(("hw", t - 2)) + 1)
                for m in (2 * sixth, 2 * sixth + 1):
                    k = m // 3
                    a, w = ((nTh, wgh), (nTl, wgh), (nTh, wgl))[m % 3]
                    ins = pe.matmul(bank[6 + t % 2][:, :], a[:, t % 2, k, :], w[:, k, :],
                                    start=m == 0, stop=m == 3 * K - 1)
                if sixth == 5:
                    ins.then_inc(S["hw_ready"], 1)

            def sweep(n, first):
                for g in range(NG):
                    q, k = divmod(g, BG)
                    if k == 0:
                        pe.wait_ge(S["stat_done"], n * NB + (q + 1))
                        pe.wait_ge(S["rest_done"], n * NB + (q + 1))
                        pe.wait_ge(S["second_done"], n * NB + (q + 1))
                    pe.wait_ge(S["mov_ready"], n * NG + (g + 1))
                    if g >= HB:
                        pe.wait_ge(S["add_done"], n * NG + (g - HB + 1))
                    m = 0
                    for i in range(GRP):
                        for part in range(3):
                            t = GRP * k + i
                            ins = pe.matmul(bank[2 + g % HB][:, 0:WC], statn[:, q % 3, part, t // IL, :, t % IL],
                                            moving[:, k, :, i], start=m == 0, stop=m == 3 * GRP - 1)
                            m += 1
                    ins.then_inc(S["grp_done"], 1)
                    t, i = divmod(g, 2 * BG)
                    if first and g in (1, 3):
                        x_transposes(g // 2, 0)
                        x_transposes(g // 2, 2)
                    if first and t == 0 and i >= 4:
                        for sixth in ((0, 1), (2, 3), (4,), (5,))[i - 4]:
                            x_product(0, sixth)
                    if first and t:
                        if i in (2, 3):
                            if t + 1 < NT:
                                x_transposes(t + 1, (i - 2) * 2)
                        else:
                            i = i if i < 2 else i - 2
                            if (t, i) < (NT - 1, 4):
                                x_product(t, i)

            sweep(0, True)
            x_product(NT - 1, 4)
            x_product(NT - 1, 5)
            pe.wait_ge(S["nbody_done"], 1)
            sweeps = pe.value_load(nbody[0:1, 0:1], min_val=1, max_val=N // WIN + 1)
            with pe.If(sweeps > 1):
                with pe.Fori(1, sweeps) as n:
                    sweep(n, False)

            def a_transposes(use):
                _, cb, h = use
                b = t_begin(use)
                v = adj[:, cb * P * SH:(cb + 1) * P * SH].rearrange("r (c s) -> r s c", s=SH)
                for s in range(HT):
                    ins = pe.transpose(b[:, s * P:(s + 1) * P], v[:, h * HT + s], ident[:, :])
                ins.then_inc(S["tr_ready"], 1)

            def gnn_step(t, cb, first, last):
                s = t % HT
                m = 0
                for a, bb in ((aTh, hwh), (aTl, hwh), (aTh, hwl)):
                    ins = pe.matmul(abank(("gnn", t))[:, :], a[:, cb, s * P:(s + 1) * P], bb[:, cb, :],
                                    start=first and m == 0, stop=last and m == 2)
                    m += 1
                return ins

            pe.wait_ge(S["nbody_done"], 2)
            a_transposes(("a", 0, 0))
            a_transposes(("a", 1, 0))
            for t in range(HT):
                a_begin(("gnn", t))
            for cb in range(NT):
                pe.wait_ge(S["tr_done"], LO.index(("a", cb, 0)) + 1)
                pe.wait_ge(S["raw_rest"], R.index(("hw", cb)) + 1)
                for t in range(HT):
                    ins = gnn_step(t, cb, cb == 0, cb == NT - 1)
                    if cb == NT - 1:
                        ins.then_inc(S["acc_ready"], 1)
                        if t == HT - 1:
                            pe.nop().then_inc(S["cb_done"], 1)
                    elif t == HT - 1:
                        ins.then_inc(S["cb_done"], 1)
                if cb + 2 < NT:
                    a_transposes(("a", cb + 2, 0))
                a_transposes(("a", cb, 1))

            def n_transposes(t):
                b = t_begin(("n", t))
                pe.wait_ge(S["xn2_done"], t + 1)
                v = xn2[:, t % HT, :].rearrange("r (p k) -> r k p", k=K)
                for k in range(K):
                    ins = pe.transpose(b[:, k * P:(k + 1) * P], v[:, k], ident[:, :])
                ins.then_inc(S["tr_ready"], 1)

            def logits_transposed(h):
                b = t_begin(("lgT", h))
                if h == 0:
                    pe.wait_ge(S["split_hi"], 2 * K)
                pe.wait_ge(S["tr_done"], LO.index(("n", h * HT + HT - 1)) + 1)
                for k in range(K):
                    w = wrg2[:, k, :, :].rearrange("p s e -> p (s e)")
                    pe.matmul(b[0:10 * G, :], w, xTh[:, h, k, :], start=k == 0, stop=False)
                    ins = pe.matmul(b[0:10 * G, :], w, xTl[:, h, k, :], start=False, stop=k == K - 1)
                ins.then_inc(S["tr_ready"], 1)

            def logits(h):
                b = t_begin(("logits", h))
                pe.wait_ge(S["lgT_done"], h + 1)
                for s in range(HT):
                    ins = pe.transpose(b[:, s * 64:s * 64 + 10 * G], lgT[:, s * P:(s + 1) * P],
                                       ident[0:10 * G, 0:10 * G])
                ins.then_inc(S["tr_ready"], 1)

            def hidden_product(name, h, j):
                wh, wl = (w1h, w1l) if name == "h1" else (w3h, w3l)
                b = a_begin((name, h, j))
                c = slice(j * P, (j + 1) * P)
                split_product(b[:, :], [(wh[:, k, c], wl[:, k, c], xTh[:, h, k, :], xTl[:, h, k, :])
                                        for k in range(K)]).then_inc(S["acc_ready"], 1)

            def tw_transposes(h):
                b = t_begin(("tw", h))
                pe.wait_ge(S["tw_done"], 2 * HT * (h + 1))
                for s in range(HT):
                    ins = pe.transpose(b[0:E2, s * P:(s + 1) * P], tw[:, s, :], ident[:, :])
                ins.then_inc(S["tr_ready"], 1)

            def tw_rows(h, j):
                b = a_begin(("tw", h, j))
                if j == 0:
                    pe.wait_ge(S["tr_done"], LO.index(("tw", h)) + 1)
                pe.matmul(b[:, :], expand[:, j, :], twT[:, :], start=True, stop=True).then_inc(S["acc_ready"], 1)

            def output(h):
                if h == 0:
                    pe.wait_ge(S["split_lo"], 3 * K)
                for t0 in (h * HT, h * HT + 2):
                    banks = [a_begin(("y", t)) for t in (t0, t0 + 1)]
                    for js in (range(K - 1), (K - 1,)):
                        if t0 == h * HT:
                            pe.wait_ge(S["g_lo"], h * K + js[-1] + 1)
                        for i in range(2):
                            r = slice((t0 + i) % HT * P, ((t0 + i) % HT + 1) * P)
                            for j in js:
                                for m, (a, w) in enumerate(((gTh, w2h), (gTl, w2h), (gTh, w2l))):
                                    ins = pe.matmul(banks[i][:, :], a[:, j, r], w[:, j, :],
                                                    start=j == 0 and m == 0, stop=j == K - 1 and m == 2)
                            if js[-1] == K - 1:
                                ins.then_inc(S["acc_ready"], 1)

            for t in range(HT, NT):
                a_begin(("gnn", t))
                for cb in range(NT):
                    if t == HT:
                        pe.wait_ge(S["tr_done"], LO.index(("a", cb, 1)) + 1)
                    ins = gnn_step(t, cb, cb == 0, cb == NT - 1)
                    if t == NT - 1 and cb == NT // 2 - 1:
                        n_transposes(2)
                        n_transposes(3)
                ins.then_inc(S["acc_ready"], 1)
                if t == NT - 2:
                    n_transposes(0)
                    n_transposes(1)
            logits_transposed(0)
            pe.wait_ge(S["split_lo"], 2 * K)
            hidden_product("h1", 0, 0)
            logits(0)
            hidden_product("h3", 0, 0)
            for j in range(1, K):
                hidden_product("h1", 0, j)
                if j >= 2:
                    n_transposes(2 * j)
                    n_transposes(2 * j + 1)
                hidden_product("h3", 0, j)
            tw_transposes(0)
            logits_transposed(1)
            pe.wait_ge(S["c_expand"], 2)
            for j in range(K):
                tw_rows(0, j)
            hidden_product("h1", 1, 0)
            logits(1)
            hidden_product("h3", 1, 0)
            output(0)
            hidden_product("h1", 1, 1)
            tw_transposes(1)
            hidden_product("h3", 1, 1)
            tw_rows(1, 0)
            tw_rows(1, 1)
            hidden_product("h1", 1, 2)
            hidden_product("h3", 1, 2)
            tw_rows(1, 2)
            hidden_product("h1", 1, 3)
            tw_rows(1, 3)
            hidden_product("h3", 1, 3)
            output(1)

        @block.vector
        def _(v):
            step = [0]

            def link(ins):
                step[0] += 1
                ins.then_inc(S["chain"], 1)
                v.wait_ge(S["chain"], step[0])

            v.memset(adj[:, 0:ADJ_V], 0.0).then_inc(S["c_adj"], 1)
            v.wait_ge(S["d_edges"], 48)
            v.tensor_scalar(lo_i[:, :], src_i[:, :], P - 1, None, ALU.bitwise_and).then_inc(S["prep"], 1)
            v.tensor_scalar(hi_i[:, :], src_i[:, :], 7, None, ALU.logical_shift_right).then_inc(S["prep"], 1)
            v.wait_ge(S["prep"], 2)
            v.tensor_copy(lo_f[:, :], lo_i[:, :]).then_inc(S["prep"], 1)
            v.scalar_tensor_tensor(comb[:, :], dst_i[:, :], float(SH), hi_i[:, :], ALU.mult, ALU.add).then_inc(S["prep"], 1)
            v.wait_ge(S["d_dstg"], 16)
            v.tensor_reduce(gmm[:, 0:1], dst_g[:, :], AX_X, ALU.min)
            link(v.tensor_reduce(gmm[:, 1:2], dst_g[:, :], AX_X, ALU.max))
            v.wait_ge(S["c_ident"], 1)
            for s in range(2):
                v.tensor_scalar(gdiag[:, s, :], ident[0:NG, 0:NG], gmm[:, s:s + 1], None, ALU.mult).then_inc(S["gdiag_done"], 1)

            def row_stats(t):
                v.bn_stats(stats[:, t, :], x_sb[:, t, :]).then_inc(S["chain"], 1)
                step[0] += 1
                v.wait_ge(S["chain"], step[0])
                return v.bn_aggr(mv[:, t, :], stats[:, t, :])

            def roots(i):
                v.wait_ge(S["std_done"], i + 1)
                r = slice(*ROOTS[i])
                link(v.reciprocal(rstd[:, r], std[:, r]))
                if i in (1, 2):
                    v.scalar_tensor_tensor(bias_n[:, r], mv[:, r, 0], -1.0, rstd[:, r], ALU.mult, ALU.mult)\
                        .then_inc(S["norm_ready"], 1)

            def tr_rest(use, dst_lo, src_psum, hi):
                v.wait_ge(S["tr_hi"], HI.index(use) + 1)
                return v.tensor_tensor(dst_lo, src_psum, hi.bitcast(F32), ALU.subtract).then_inc(S["tr_done"], 1)

            def statistics(i):
                for t in range(*ROOTS[i]):
                    v.wait_ge(d_x[t], 16)
                    ins = row_stats(t)
                ins.then_inc(S["std_req"], 1)

            def center():
                v.tensor_scalar(column[:, :], combrel[:, :], float(-WC // 2), None, ALU.add).then_inc(S["centered"], 1)

            def mark(ins):
                step[0] += 1
                ins.then_inc(S["chain"], 1)
                return step[0]

            def edges():
                eb, bb = tbank("edges"), tbank("base")
                v.wait_ge(S["tr_ready"], 1)
                v.tensor_copy(src_lo[:, :], eb[:, 0:P])
                whole = mark(v.tensor_copy(w_res[:, 0, :], eb[:, 2 * P:3 * P]))
                v.wait_ge(S["tr_ready"], 2)
                based = mark(v.tensor_scalar(base8[:, :], bb[:, 0:NG], float(SH), None, ALU.mult))
                v.wait_ge(S["chain"], whole)
                part0 = mark(v.tensor_copy(w_parts[:, 0, :], w_res[:, 0, :]))
                v.wait_ge(S["chain"], based)
                v.tensor_tensor(combrel[:, :].rearrange("p (g i) -> p g i", i=GRP),
                                eb[:, P:2 * P].rearrange("p (g i) -> p g i", i=GRP),
                                base8[:, :].unsqueeze(2).broadcast_to([P, NG, GRP]), ALU.subtract).then_inc(S["tr_done"], 1)
                v.wait_ge(S["chain"], part0)
                rest1 = mark(v.tensor_tensor(w_res[:, 1, :], w_res[:, 0, :], w_parts[:, 0, :], ALU.subtract))
                v.tensor_copy(offs[:, :], base8[0:1, :])
                gmaxed = mark(v.tensor_copy(gmax_row[:, :], bb[0:1, NG:2 * NG]))
                v.wait_ge(S["chain"], rest1)
                part1 = mark(v.tensor_copy(w_parts[:, 1, :], w_res[:, 1, :]))
                v.wait_ge(S["chain"], gmaxed)
                v.tensor_tensor(span[:, :], gmax_row[:, :], bb[0:1, 0:NG], ALU.subtract).then_inc(S["tr_done"], 1)
                v.wait_ge(S["tr_done"], 1)
                center()
                v.wait_ge(S["chain"], part1)
                v.tensor_tensor(w_res[:, 2, :], w_res[:, 1, :], w_parts[:, 1, :], ALU.subtract).then_inc(S["parts_done"], 1)

            def count_sweeps():
                v.wait_ge(S["tr_done"], 2)
                link(v.tensor_reduce(spanm[:, :], span[:, :], AX_X, ALU.max))
                v.wait_ge(S["c_kwin"], 1)
                link(v.tensor_scalar(kcmp[:, :], kwin[:, :], spanm[:, 0:1], None, ALU.is_le))
                link(v.tensor_reduce(nwin[:, :], kcmp[:, :], AX_X, ALU.add))
                link(v.tensor_scalar(nbody[:, :], nwin[:, :], 1.0, None, ALU.mult))
                v.engine_nop().then_inc(S["nbody_done"], 1)

            def normalize(t):
                v.tensor_scalar(xn1[:, t % 2, :], x_sb[:, t, :], mv[:, t, 0:1], rstd[:, t:t + 1],
                                ALU.subtract, ALU.mult).then_inc(S["xn_done"], 1)

            def onehots(b):
                v.tensor_tensor(onehot[:, b], iota_lo[:, :, :].unsqueeze(1).broadcast_to([P, BT // IL, P, IL]),
                                over_columns(src_lo[:, b * BT:(b + 1) * BT]), ALU.is_equal).then_inc(S["onehot_done"], 1)

            def parts(b, slot):
                v.tensor_tensor(statn[:, slot, 0], onehot[:, b], over_columns(w_parts[:, 0, b * BT:(b + 1) * BT]),
                                ALU.mult).then_inc(S["stat_done"], 1)

            def windows(q, columns):
                columns[BG * q:BG * (q + 1)] = nc.values_load_multi_w_load_instructions(
                    offs[0:1, BG * q:BG * (q + 1)], engines=[mybir.EngineType.DVE], min_val=0, max_val=NC)[1]

            def stationaries(q, first, columns):
                if first:
                    if q == 0:
                        onehots(0)
                    if q + 1 < NB:
                        onehots(q + 1)
                    v.wait_ge(S["onehot_done"], q + 1)
                parts(q, q % 3)
                windows(q, columns)

            def sweep(n, first, columns):
                def add(g):
                    v.wait_ge(S["grp_done"], n * NG + (g + 1))
                    if first and g == 0:
                        v.wait_ge(S["c_adj"], 2)
                    if g:
                        v.wait_ge(S["add_done"], n * NG + g)
                    a = adj[:, bass.ds(columns[g], WC)]
                    v.tensor_tensor(a, a, bank[2 + g % HB][:, 0:WC], ALU.add).then_inc(S["add_done"], 1)

                if not first:
                    v.tensor_scalar(combrel[:, :], combrel[:, :], float(-WC), None, ALU.add).then_inc(S["shifted"], 1)
                    v.tensor_scalar(offs[:, :], offs[:, :], float(WC), float(NC), ALU.add, ALU.min).then_inc(S["shifted"], 1)
                    v.wait_ge(S["shifted"], n * 2)
                    center()
                    v.wait_ge(S["centered"], n + 1)
                    stationaries(0, first, columns)
                for q in range(NB):
                    for k in range(BG):
                        g = q * BG + k
                        v.tensor_tensor(moving[:, k], iota_win[:, :, :],
                                        column[:, GRP * g:GRP * g + GRP].unsqueeze(1).broadcast_to([P, WC, GRP]),
                                        ALU.is_equal).then_inc(S["mov_ready"], 1)
                        if g >= LAG:
                            add(g - LAG)
                        if first and g == 0:
                            roots(0)
                        if first and g in (0, 1):
                            normalize(g)
                        if g == 0:
                            stationaries(1, first, columns)
                        if k == LAG - 1 and q + 2 < NB:
                            stationaries(q + 2, first, columns)
                        if first and (q, k) == (8, 0):
                            count_sweeps()
                        if first and (q, k) == (0, 3):
                            statistics(1)
                        if first and (q, k) == (1, 1):
                            roots(1)
                        if first and 1 <= q <= 4 and k == 0:
                            v.wait_ge(d_x[q + 3], 16)
                            taken = mark(v.bn_stats(stats[:, q + 3, :], x_sb[:, q + 3, :]))
                        if first and 1 <= q <= 4 and k == 1:
                            v.wait_ge(S["chain"], taken)
                            ins = v.bn_aggr(mv[:, q + 3, :], stats[:, q + 3, :])
                            if q == 4:
                                ins.then_inc(S["std_req"], 1)
                        if first and (q, k) == (12, 1):
                            loaded.append(v.value_load(nbody[0:1, 0:1], min_val=1, max_val=N // WIN + 1))
                        if first and (q, k) == (5, 1):
                            roots(2)
                for g in range(NG - LAG, NG):
                    add(g)
                v.wait_ge(S["add_done"], n * NG + NG)

            statistics(0)
            v.wait_ge(S["c_iota"], 2)
            edges()
            v.wait_ge(S["centered"], 1)
            columns, loaded = [None] * NG, []
            stationaries(0, True, columns)
            sweep(0, True, columns)
            sweeps = loaded[0]
            with v.If(sweeps > 1):
                with v.Fori(1, sweeps) as n:
                    sweep(n, False, [None] * NG)
            v.engine_nop().then_inc(S["nbody_done"], 1)

            for u in T:
                if u[0] == "a":
                    if u[2] == 1:
                        v.wait_ge(S["cb_done"], u[1] + 1)
                    if u == ("a", 5, 0):
                        v.wait_ge(S["raw_rest"], len(R))
                    tr_rest(u, aTl[:, u[1], :], tbank(u)[:, :], aTh[:, u[1], :])

            v.wait_ge(S["d_small"], 16 * 5)

            def gnn_out(t):
                v.wait_ge(S["acc_ready"], A.index(("gnn", t)) + 1)
                ins = v.tensor_tensor(relu_in[:, t % 2, :], abank(("gnn", t))[:, :], biasb[:, :], ALU.add)
                ins.then_inc(S["acc_free"], 1)
                v.wait_ge(S["acc_free"], t + 1)
                link(v.scalar_tensor_tensor(x_sb[:, t, :], relu_in[:, t % 2, :], 0.0, x_sb[:, t, :], ALU.max, ALU.add))
                ins = row_stats(t)
                if t % HT == HT - 1:
                    ins.then_inc(S["std_req"], 1)

            def normalize2(t):
                if t >= HT:
                    v.wait_ge(S["tr_ready"], T.index(("n", t - HT)) + 1)
                v.tensor_scalar(xn2[:, t % HT, :], x_sb[:, t, :], mv[:, t, 0:1], rstd[:, t:t + 1],
                                ALU.subtract, ALU.mult).then_inc(S["xn2_done"], 1)

            def n_rest(t):
                r = slice(t % HT * P, (t % HT + 1) * P)
                tr_rest(("n", t), xTl[:, t // HT, :, r], tbank(("n", t))[:, :].rearrange("p (k r) -> p k r", k=K),
                        xTh[:, t // HT, :, r])

            def routing(h):
                v.wait_ge(S["tr_ready"], T.index(("logits", h)) + 1)
                lb = tbank(("logits", h))[:, 0:HT * 64].rearrange("p (s a) -> p s a", s=HT)
                l = lg[:, :, :].rearrange("p (s a) e -> p s (a e)", s=HT)
                link(v.tensor_tensor(l, lb[:, :, 0:5 * G], brg[:, :].unsqueeze(1).broadcast_to([P, HT, 5 * G]), ALU.add))
                v.tensor_tensor(l, lb[:, :, 5 * G:10 * G], l, ALU.add).then_inc(S["tr_done"], 1)
                v.wait_ge(S["tr_done"], LO.index(("logits", h)) + 1)

                def over(a):
                    return a[:, :].unsqueeze(2).broadcast_to([P, NGR, G])

                link(v.tensor_reduce(gm[:, :], lg[:, :, :], AX_X, ALU.max))
                v.tensor_tensor(gc[:, :, :], lg[:, :, :], over(gm), ALU.subtract).then_inc(S["exp_req"], 1)
                v.wait_ge(S["exp_done"], h + 1)
                link(v.tensor_reduce(gs[:, :], ge[:, :, :], AX_X, ALU.add))
                link(v.reciprocal(gr[:, :], gs[:, :]))
                link(v.tensor_tensor(gp[:, :, :], ge[:, :, :], over(gr), ALU.mult))
                pj = gp[:, :, :].unsqueeze(2).broadcast_to([P, NGR, G, G])
                pi = gp[:, :, :].unsqueeze(3).broadcast_to([P, NGR, G, G])
                v.tensor_tensor(gt[:, :, :, :], pj, pi, ALU.is_gt)
                link(v.tensor_tensor(eq[:, :, :, :], pj, pi, ALU.is_equal))
                link(v.tensor_tensor(eq[:, :, :, :].rearrange("p a i j -> p a (i j)"),
                                     eq[:, :, :, :].rearrange("p a i j -> p a (i j)"),
                                     tie[:, :, :].rearrange("p i j -> p (i j)").unsqueeze(1).broadcast_to([P, NGR, G * G]),
                                     ALU.mult))
                link(v.tensor_tensor(gt[:, :, :, :], gt[:, :, :, :], eq[:, :, :, :], ALU.add))
                link(v.tensor_reduce(rank[:, :, :], gt[:, :, :, :], AX_X, ALU.add))
                link(v.scalar_tensor_tensor(p2[:, :, :], rank[:, :, :], 1.0, gp[:, :, :], ALU.is_le, ALU.mult))
                link(v.tensor_reduce(gs[:, :], p2[:, :, :], AX_X, ALU.add))
                link(v.tensor_scalar(gr[:, :], gs[:, :], 0.9, None, ALU.is_le))
                link(v.tensor_tensor(m2[:, :, :], rank[:, :, :], over(gr), ALU.is_le))
                link(v.tensor_tensor(p2[:, :, :], gp[:, :, :], m2[:, :, :], ALU.mult))
                link(v.tensor_reduce(gs[:, :], p2[:, :, :], AX_X, ALU.add))
                link(v.tensor_scalar(gs[:, :], gs[:, :], 1e-9, None, ALU.add))
                link(v.reciprocal(gr[:, :], gs[:, :]))
                link(v.tensor_tensor(p2[:, :, :], p2[:, :, :], over(gr), ALU.mult))
                w5 = p2[:, :, :].rearrange("p (s a) e -> p s a e", s=HT)
                for s in range(HT):
                    wg = w5[:, s, 0, :].unsqueeze(2).broadcast_to([P, G, G])
                    for c in (0, 32):
                        v.scalar_tensor_tensor(tw[:, s, c:c + E].rearrange("p (g e) -> p g e", g=G), w5[:, s, 1:5, :],
                                               0.5, wg, ALU.mult, ALU.mult).then_inc(S["tw_done"], 1)

            def hide(h, j):
                u = factors(h, j)[0]
                v.wait_ge(S["silu_done"], K * h + j + 1)
                v.wait_ge(S["acc_ready"], A.index(u) + 1)
                v.tensor_tensor(hidden[:, j, :], silu[:, j, :], abank(u)[:, :], ALU.mult).then_inc(S["acc_free"], 2)

            def gate(h, j):
                u1, u = factors(h, j)
                v.wait_ge(S["acc_ready"], A.index(u) + 1)
                v.wait_ge(S["acc_free"], A.index(u1) + 1)
                v.tensor_tensor(gated[:, j, :], hidden[:, j, :], abank(u)[:, :], ALU.mult).then_inc(S["acc_free"], 1)
                v.wait_ge(S["acc_free"], A.index(u) + 1)
                v.engine_nop().then_inc(S["gated_done"], 1)

            def gate_rest(h, j):
                v.wait_ge(S["g_hi"], K * h + j + 1)
                v.tensor_tensor(gTl[:, j, :], gated[:, j, :], gTh[:, j, :].bitcast(F32),
                                ALU.subtract).then_inc(S["g_lo"], 1)

            def finish(t):
                u = A.index(("y", t))
                v.wait_ge(S["acc_ready"], u + 1)
                if t >= 4:
                    v.wait_ge(d_out[t % 4], 16 * (t // 4))
                v.tensor_tensor(y_sb[:, t % 4, :], abank(("y", t))[:, :], x_sb[:, t, :], ALU.add).then_inc(S["acc_free"], 1)
                v.wait_ge(S["acc_free"], u + 1)
                v.engine_nop().then_inc(S["y_done"], 1)

            for t in range(HT):
                gnn_out(t)
            roots(3)
            v.wait_ge(S["split_lo"], 2 * K)
            for t in range(HT):
                normalize2(t)
            gnn_out(HT)
            gnn_out(HT + 1)
            n_rest(0)
            n_rest(1)
            n_rest(2)
            n_rest(3)
            gnn_out(HT + 2)
            gnn_out(HT + 3)
            routing(0)
            roots(4)
            for t in range(HT, NT):
                normalize2(t)

            def tw_rest(h):
                v.wait_ge(S["tr_hi"], HI.index(("tw", h)) + 1)
                v.tensor_tensor(twT[32:E2, :], tbank(("tw", h))[32:E2, :], twT[32:E2, :].bitcast(F32),
                                ALU.subtract).then_inc(S["tr_done"], 1)

            for j in range(K):
                if j >= 2:
                    n_rest(2 * j)
                    n_rest(2 * j + 1)
                hide(0, j)
            tw_rest(0)
            for j in range(K):
                gate(0, j)
                if j:
                    gate_rest(0, j - 1)
            gate_rest(0, K - 1)
            routing(1)
            hide(1, 0)
            for t in range(HT):
                finish(t)
            tw_rest(1)
            hide(1, 1)
            gate(1, 0)
            gate(1, 1)
            gate_rest(1, 0)
            gate_rest(1, 1)
            for j in (2, 3):
                hide(1, j)
                gate(1, j)
                gate_rest(1, j)
            for t in range(HT, NT):
                finish(t)


_INS = ["x", "src", "dst", "edge_weight", "L0_gnn_W", "L0_gnn_bias", "L0_ffn_Wr", "L0_ffn_br", "L0_ffn_Wgate",
        "L0_ffn_bgate", "L0_ffn_W1", "L0_ffn_W3", "L0_ffn_W2"]


def kernel(**inputs):
    import numpy as _np
    import concourse.bacc as _bacc
    from concourse import mybir as _mybir
    from concourse.bass_utils import run_bass_kernel_spmd as _run

    nc = _bacc.Bacc("TRN2", target_bir_lowering=False, num_devices=1)
    arrays, args = {}, []
    for name in _INS:
        a = _np.ascontiguousarray(inputs[name])
        arrays[f"in_{name}_dram"] = a
        args.append(nc.dram_tensor(f"in_{name}_dram", a.shape, _mybir.dt.from_np(a.dtype), kind="ExternalInput").ap())
    args.append(nc.dram_tensor("out_0_dram", (N, D), F32, kind="ExternalOutput").ap())
    gnn_ffn(nc, *args)
    r = _run(nc, [arrays], core_ids=[0])
    return r.results[0]["out_0_dram"]
```
